# Optimizing a Trainium2 kernel written in Bass

```python
import numpy as np
import jax
import jax.numpy as jnp

def _softmax(x, axis=-1):
    return jax.nn.softmax(x, axis=axis)

def _gelu(x):
    return jax.nn.gelu(x, approximate=True)

def _silu(x):
    return jax.nn.silu(x)

def _sigmoid(x):
    return jax.nn.sigmoid(x)

def _layernorm(x, axis=-1, eps=1e-05):
    m = jnp.mean(x, axis=axis, keepdims=True)
    v = jnp.var(x, axis=axis, keepdims=True)
    return (x - m) / jnp.sqrt(v + eps)

def _scatter_add(tgt, idx, src, axis=0):
    return tgt.at[idx].add(src)

def _segment_sum(src, seg, n):
    return jax.ops.segment_sum(src, seg, n)
kernel_name = 'mk_gps_d1_gnn_r8_ea7548'

def setup_inputs(seed: int=0):
    np.random.seed(seed)
    _w = jnp.asarray

    def _rec_inputs():
        import jax
        import jax.numpy as jnp
        _gk = jax.random.key(seed)
        x = -0.0002117 + 1 * jax.random.normal(jax.random.fold_in(_gk, 1), (1250, 512), jnp.float32)
        src = jax.random.randint(jax.random.fold_in(_gk, 2), (40000,), 0, 1250, jnp.int32)
        dst = jax.random.randint(jax.random.fold_in(_gk, 3), (40000,), 0, 1250, jnp.int32)
        _o = jnp.argsort(dst, stable=True)
        src = src[_o]
        dst = dst[_o]
        return (x, src, dst)
    x, src, dst = _rec_inputs()

    def _L0_gnn_setup():
        import jax, jax.numpy as jnp
        import numpy as np
        N = 6250
        IN_CH = 512
        OUT_CH = 512
        DEG = 32
        E = N * DEG
        key = jax.random.key(seed)
        kx, kwc, kwn, kb, ke = jax.random.split(key, 5)
        x = jax.random.normal(kx, (N, IN_CH), dtype=jnp.float32)
        bound = 1.0 / np.sqrt(IN_CH)
        wc = jax.random.uniform(kwc, (IN_CH, OUT_CH), minval=-bound, maxval=bound, dtype=jnp.float32)
        wn = jax.random.uniform(kwn, (IN_CH, OUT_CH), minval=-bound, maxval=bound, dtype=jnp.float32)
        bias = jax.random.uniform(kb, (OUT_CH,), minval=-bound, maxval=bound, dtype=jnp.float32)
        src = jnp.repeat(jnp.arange(N, dtype=jnp.int64), DEG)
        dst = jax.random.randint(ke, (E,), 0, N, dtype=jnp.int64)
        edge_index = jnp.stack([src, dst], axis=0)
        return {'x': x, 'wc': wc, 'wn': wn, 'bias': bias, 'edge_index': edge_index}
    _L0_gnn_all = _L0_gnn_setup()
    _L0_gnn_in = {k: v for k, v in _L0_gnn_all.items() if k in ('wc', 'wn', 'bias')}
    del _L0_gnn_all

    def _L0_mix_setup():
        import jax, jax.numpy as jnp
        import numpy as np
        import math
        E = 512
        H = 8
        D = E // H
        M = 64
        EPS = 1e-08
        CLAMP_MAX = 50.0

        def _make_omega(key):
            w = jax.random.normal(key, (D, M), dtype=jnp.float32) / np.sqrt(D)
            q, _ = jnp.linalg.qr(w)
            return q

        def _positive_random_feature_map(v, omega):
            f = jnp.minimum(v @ omega, CLAMP_MAX)
            l2 = jnp.maximum(jnp.linalg.norm(v, axis=-1, keepdims=True), EPS)
            norm_term = jnp.maximum(jnp.exp(-0.5 * l2 * l2), EPS)
            return norm_term * jnp.exp(f)
        key = jax.random.key(seed)
        ks = jax.random.split(key, 8)
        B, S = (2, 2048)
        x = jax.random.normal(ks[0], (B, S, E), dtype=jnp.float32)
        sc = 1.0 / np.sqrt(E)
        Wq = jax.random.normal(ks[1], (E, E), dtype=jnp.float32) * sc
        Wk = jax.random.normal(ks[2], (E, E), dtype=jnp.float32) * sc
        Wv = jax.random.normal(ks[3], (E, E), dtype=jnp.float32) * sc
        Wo = jax.random.normal(ks[4], (E, E), dtype=jnp.float32) * sc
        omega_q = _make_omega(ks[5])
        omega_k = _make_omega(ks[6])
        return {'x': x, 'Wq': Wq, 'Wk': Wk, 'Wv': Wv, 'Wo': Wo, 'omega_q': omega_q, 'omega_k': omega_k}
    _L0_mix_all = _L0_mix_setup()
    _L0_mix_in = {k: v for k, v in _L0_mix_all.items() if k in ('Wq', 'Wk', 'Wv', 'Wo', 'omega_q', 'omega_k')}
    del _L0_mix_all

    def _L0_ffn_setup():
        import jax, jax.numpy as jnp
        import numpy as np
        DIM = 512
        HEADS = 8
        DIM_KEY = 32
        NUM_EXPERTS = 8192
        NUM_KEYS = 256
        TOPK = 16
        BN_EPS = 1e-05

        def peer_forward(x, w_q, keys, weight_down_embed, weight_up_embed):
            b, n, _ = x.shape
            q = x @ w_q * (1.0 / np.sqrt(1.0 + BN_EPS))
            queries = q.reshape(b, n, 2, HEADS, DIM_KEY).transpose(2, 0, 1, 3, 4)
            sim = jnp.einsum('pbnhd,hkpd->pbnhk', queries, keys)
            v0, i0 = jax.lax.top_k(sim[0], TOPK)
            v1, i1 = jax.lax.top_k(sim[1], TOPK)
            all_scores = v0[..., :, None] + i0[..., None, :].astype(v0.dtype)
            all_scores = all_scores.reshape(*all_scores.shape[:-2], -1)
            scores, pk_indices = jax.lax.top_k(all_scores, TOPK)
            weights_down = jnp.take(weight_down_embed, pk_indices, axis=0)
            weights_up = jnp.take(weight_up_embed, pk_indices, axis=0)
            h = jnp.einsum('bnd,bnhkd->bnhk', q, weights_down)
            h = jax.nn.gelu(h)
            h = h * jax.nn.softmax(scores, axis=-1)
            out = jnp.einsum('bnhk,bnhkd->bnd', h, weights_up)
            return out
        key = jax.random.key(seed)
        k1, k2, k3, k4, k5 = jax.random.split(key, 5)
        b, n = (2, 512)
        x = jax.random.normal(k1, (b, n, DIM), dtype=jnp.float32)
        w_q = jax.random.normal(k2, (DIM, DIM_KEY * HEADS * 2), dtype=jnp.float32) / np.sqrt(DIM)
        keys = jax.random.normal(k3, (HEADS, NUM_KEYS, 2, DIM_KEY), dtype=jnp.float32) * 0.01
        weight_down_embed = jax.random.normal(k4, (NUM_EXPERTS, DIM), dtype=jnp.float32) * 0.01
        weight_up_embed = jax.random.normal(k5, (NUM_EXPERTS, DIM), dtype=jnp.float32) * 0.01
        return {'x': x, 'w_q': w_q, 'keys': keys, 'weight_down_embed': weight_down_embed, 'weight_up_embed': weight_up_embed}
    _L0_ffn_all = _L0_ffn_setup()
    _L0_ffn_in = {k: v for k, v in _L0_ffn_all.items() if k in ('w_q', 'keys', 'weight_down_embed', 'weight_up_embed')}
    del _L0_ffn_all
    return {'x': x, 'src': src, 'dst': dst, 'L0_gnn_wc': _L0_gnn_in['wc'], 'L0_gnn_wn': _L0_gnn_in['wn'], 'L0_gnn_bias': _L0_gnn_in['bias'], 'L0_mix_Wq': _L0_mix_in['Wq'], 'L0_mix_Wk': _L0_mix_in['Wk'], 'L0_mix_Wv': _L0_mix_in['Wv'], 'L0_mix_Wo': _L0_mix_in['Wo'], 'L0_mix_omega_q': _L0_mix_in['omega_q'], 'L0_mix_omega_k': _L0_mix_in['omega_k'], 'L0_ffn_w_q': _L0_ffn_in['w_q'], 'L0_ffn_keys': _L0_ffn_in['keys'], 'L0_ffn_weight_down_embed': _L0_ffn_in['weight_down_embed'], 'L0_ffn_weight_up_embed': _L0_ffn_in['weight_up_embed']}

def reference(x, src, dst, L0_gnn_wc, L0_gnn_wn, L0_gnn_bias, L0_mix_Wq, L0_mix_Wk, L0_mix_Wv, L0_mix_Wo, L0_mix_omega_q, L0_mix_omega_k, L0_ffn_w_q, L0_ffn_keys, L0_ffn_weight_down_embed, L0_ffn_weight_up_embed):
    import jax
    import jax.numpy as jnp

    def _L0_gnn_ref(x, wc, wn, bias, edge_index):
        import jax, jax.numpy as jnp
        import numpy as np
        N = 6250
        IN_CH = 512
        OUT_CH = 512
        DEG = 32
        E = N * DEG
        alpha = x @ wc
        beta = x @ wn
        src, dst = (edge_index[0], edge_index[1])
        sums = jax.ops.segment_sum(beta[dst], src, num_segments=x.shape[0])
        counts = jax.ops.segment_sum(jnp.ones_like(src, dtype=beta.dtype), src, num_segments=x.shape[0])
        gamma = sums / counts[:, None]
        return alpha + gamma + bias

    def _L0_mix_ref(x, Wq, Wk, Wv, Wo, omega_q, omega_k):
        import jax, jax.numpy as jnp
        import numpy as np
        import math
        E = 512
        H = 8
        D = E // H
        M = 64
        EPS = 1e-08
        CLAMP_MAX = 50.0

        def _make_omega(key):
            w = jax.random.normal(key, (D, M), dtype=jnp.float32) / np.sqrt(D)
            q, _ = jnp.linalg.qr(w)
            return q

        def _positive_random_feature_map(v, omega):
            f = jnp.minimum(v @ omega, CLAMP_MAX)
            l2 = jnp.maximum(jnp.linalg.norm(v, axis=-1, keepdims=True), EPS)
            norm_term = jnp.maximum(jnp.exp(-0.5 * l2 * l2), EPS)
            return norm_term * jnp.exp(f)
        B, S, _ = x.shape
        scale = 1.0 / np.sqrt(D)

        def heads(y):
            return y.reshape(B, S, H, D).transpose(0, 2, 1, 3)
        Q = heads(x @ Wq) * scale
        K = heads(x @ Wk) * scale
        V = heads(x @ Wv)
        Q_phi = _positive_random_feature_map(Q, omega_q)
        K_phi = _positive_random_feature_map(K, omega_k)
        KV = jnp.einsum('bhsm,bhsd->bhmd', K_phi, V)
        QKV = jnp.einsum('bhsm,bhmd->bhsd', Q_phi, KV)
        K_ones = K_phi.sum(axis=2)
        QK_ones = jnp.einsum('bhsm,bhm->bhs', Q_phi, K_ones)
        attn = QKV / QK_ones[..., None]
        out = attn.transpose(0, 2, 1, 3).reshape(B, S, E)
        return out @ Wo

    def _L0_ffn_ref(x, w_q, keys, weight_down_embed, weight_up_embed):
        import jax, jax.numpy as jnp
        import numpy as np
        DIM = 512
        HEADS = 8
        DIM_KEY = 32
        NUM_EXPERTS = 8192
        NUM_KEYS = 256
        TOPK = 16
        BN_EPS = 1e-05

        def peer_forward(x, w_q, keys, weight_down_embed, weight_up_embed):
            b, n, _ = x.shape
            q = x @ w_q * (1.0 / np.sqrt(1.0 + BN_EPS))
            queries = q.reshape(b, n, 2, HEADS, DIM_KEY).transpose(2, 0, 1, 3, 4)
            sim = jnp.einsum('pbnhd,hkpd->pbnhk', queries, keys)
            v0, i0 = jax.lax.top_k(sim[0], TOPK)
            v1, i1 = jax.lax.top_k(sim[1], TOPK)
            all_scores = v0[..., :, None] + i0[..., None, :].astype(v0.dtype)
            all_scores = all_scores.reshape(*all_scores.shape[:-2], -1)
            scores, pk_indices = jax.lax.top_k(all_scores, TOPK)
            weights_down = jnp.take(weight_down_embed, pk_indices, axis=0)
            weights_up = jnp.take(weight_up_embed, pk_indices, axis=0)
            h = jnp.einsum('bnd,bnhkd->bnhk', q, weights_down)
            h = jax.nn.gelu(h)
            h = h * jax.nn.softmax(scores, axis=-1)
            out = jnp.einsum('bnhk,bnhkd->bnd', h, weights_up)
            return out
        return peer_forward(x, w_q, keys, weight_down_embed, weight_up_embed)
    edge_index = jnp.stack([src, dst])
    xn = _layernorm(x, axis=-1)
    x = x + _L0_gnn_ref(xn, L0_gnn_wc, L0_gnn_wn, L0_gnn_bias, edge_index) + _L0_mix_ref(xn[None], L0_mix_Wq, L0_mix_Wk, L0_mix_Wv, L0_mix_Wo, L0_mix_omega_q, L0_mix_omega_k)[0]
    x = x + _L0_ffn_ref(_layernorm(x, axis=-1)[None], L0_ffn_w_q, L0_ffn_keys, L0_ffn_weight_down_embed, L0_ffn_weight_up_embed)[0]
    return x

_drawn_inputs = setup_inputs


def setup_inputs(seed=0):
    import zlib

    import numpy as np

    out = dict(_drawn_inputs(seed))
    spreads = {}
    factors = {'L0_gnn_bias': 2.726,
     'L0_mix_Wq': 8.0,
     'L0_mix_Wk': 8.0,
     'L0_mix_omega_q': 8.0,
     'L0_mix_omega_k': 8.0,
     'L0_ffn_w_q': 8.0,
     'L0_ffn_keys': 8.0,
     'L0_ffn_weight_down_embed': 8.0,
     'L0_ffn_weight_up_embed': 8.0}
    for name, (base, spread) in spreads.items():
        noise = np.random.default_rng([zlib.crc32(name.encode()), seed]).standard_normal(out[name].shape)
        drawn = base * np.exp(spread * noise) if base else spread * noise
        out[name] = jnp.asarray(drawn.astype(out[name].dtype))
    for name, factor in factors.items():
        out[name] = (out[name] * factor).astype(out[name].dtype)
    return out
```

```python
import concourse.bass as bass
from concourse import mybir
from contextlib import ExitStack

FP32 = mybir.dt.float32
FP16 = mybir.dt.float16
I32 = mybir.dt.int32
U32 = mybir.dt.uint32
ALU = mybir.AluOpType
ACT = mybir.ActivationFunctionType
AX = mybir.AxisListType


def hold(eng, sem, value, passed):
    eng.wait_ge(sem, value)
    eng.sem_inc(passed, 1)


class Steps:

    def __init__(self, eng, sem, base=0, passed=None):
        self.eng, self.sem, self.base, self.n, self.passed = eng, sem, base, 0, passed

    def link(self, ins):
        self.n += 1
        ins.then_inc(self.sem, 1)
        if self.passed is None:
            self.eng.wait_ge(self.sem, self.base + self.n)
        else:
            hold(self.eng, self.sem, self.base + self.n, self.passed)


def gps_layer(nc, x, src, dst, wc, wn, bias, Wq, Wk, Wv, Wo, om_q, om_k, wf, keys, w_down, w_up, out):
    N, D = x.shape
    E = src.shape[0]
    P = 125
    T = N // P
    KC = D // 128
    H = 8
    DH = D // H
    NPAIR = H // 2
    VC = 2 * DH + 1
    CT = 4
    NCH = E // P // CT
    FH = keys.shape[0]
    NK = keys.shape[1]
    DK = keys.shape[3]
    TOP = 16
    NE = TOP * TOP
    EC = NE // 128
    Q_SCALE = 1.0 / DH ** 0.5
    BN_SCALE = 1.0 / (1.0 + 1e-5) ** 0.5
    LN_EPS = 1e-5
    EPS = 1e-8
    CLAMP = 50.0
    LOWEST = -3.0e38
    GELU_C = 0.7978845608028654
    GELU_A = 0.044715
    banks = [(0, 512), (512, 1024), (1024, N)]

    ctx = ExitStack()
    with ctx:
        def sb(name, shape, dt=FP32):
            return ctx.enter_context(nc.sbuf_tensor(name, shape, dt))

        def sem(name):
            return ctx.enter_context(nc.semaphore(name))

        ident = sb("ident", [128, 128])
        pair_ones = sb("pair_ones", [128, 128])
        iota = sb("iota", [P, N], FP16)
        zrow = sb("zrow", [1, 512], FP16)
        om_qb = sb("om_qb", [128, 128])
        om_kb = sb("om_kb", [128, 128])
        acc = sb("acc", [P, T, D])
        beta = sb("beta", [128, T, D])
        W = sb("W", [128, 4, KC, D])
        wf_sb = sb("wf_sb", [128, KC, D])
        wu_sb = sb("wu_sb", [128, EC, D])
        wdT = sb("wdT", [128, KC, NE])
        keysT = sb("keysT", [128, 2, NK])
        bias_bc = sb("bias_bc", [P, D])
        xnT = sb("xnT", [128, 5000])
        big = sb("big", [128, T * N])
        hot = sb("hot", [P, CT * (N + P) // 2])
        w_pair = sb("w_pair", [128, 2, KC, 128])
        x_stage = sb("x_stage", [128, KC, P])
        kv_blk = sb("kv_blk", [128, 128])
        ones_blk = sb("ones_blk", [128, 128])
        edges_i = sb("edges_i", [NCH, 2, CT * P], I32)
        edges_f = sb("edges_f", [NCH, 2, CT * P])
        edge_cols = sb("edge_cols", [P, 2, NCH * CT])
        ch_lim = sb("ch_lim", [NCH, 2])
        ch_rank = sb("ch_rank", [NCH, 2])
        blk_lo = sb("blk_lo", [NCH, T])
        blk_hi = sb("blk_hi", [NCH, T])
        touch = sb("touch", [NCH, 3, T])
        cand = sb("cand", [NCH, 2, T])
        cand_max = sb("cand_max", [2 * T, 1])
        rng = sb("rng", [1, 8, T])
        rng_i = sb("rng_i", [1, 3, T], I32)
        scr_edge = sb("scr_edge", [P, 2, CT])
        iota_blk = sb("iota_blk", [P, P], FP16)
        st = sb("st", [P, T, 6])
        ag = sb("ag", [P, T, 2])
        rstd = sb("rstd", [P, T])
        mhalf = sb("mhalf", [P, T])
        nk = sb("nk", [P, T, 2])
        rcnt = sb("rcnt", [P, 1])
        ones1 = sb("ones1", [P, 2])

        xnT3 = xnT[:, 0:KC * N].rearrange("p (k n) -> p k n", k=KC)
        Wv_sb, wn_sb, wc_sb, Wo_sb = (W[:, i] for i in range(4))
        AT = big[0:P, :].rearrange("p (t n) -> p t n", t=T)
        qT, kT, sqq, sqk, qphi = (big[:, i * N:(i + 1) * N] for i in range(5))
        vaug = big[0:P, 5 * N:5 * N + T * NPAIR * VC].rearrange("p (t c v) -> p t c v", t=T, c=NPAIR)
        hot16 = hot[:, :].bitcast(FP16)
        hot_src = hot16[:, 0:CT * N].rearrange("p (k n) -> p k n", k=CT)
        hot_dst = hot16[:, CT * N:CT * (N + P)].rearrange("p (k n) -> p k n", k=CT)
        kphi = hot[:, 0:T * 128].rearrange("p (t m) -> p t m", t=T)
        xn_tile = hot[:, 0:D]
        xa_tile = hot[:, D:2 * D]
        wd_nat = beta[:, 0:EC, :]
        keys_nat = beta[:, EC, :].rearrange("p (g h d) -> p g h d", g=2, h=FH)
        ffn = W[:, 0:4].rearrange("p a k d -> p (a k d)")
        sim, allsc, rest, ex1 = (ffn[0:P, i * FH * NK:(i + 1) * FH * NK].rearrange("p (h e) -> p h e", h=FH)
                                 for i in range(4))
        ex2 = xnT[0:P, 0:FH * NK].rearrange("p (h e) -> p h e", h=FH)
        o = FH * NK

        def cut(n, rows=128):
            nonlocal o
            o += n
            return xnT[0:rows, o - n:o]

        xn2T = cut(KC * P).rearrange("p (k n) -> p k n", k=KC)
        q2T = cut(KC * P).rearrange("p (k n) -> p k n", k=KC)
        comT = cut(EC * P).rearrange("p (k n) -> p k n", k=EC)
        hx, hu, gl, sel, com = (cut(NE, P) for _ in range(5))
        AT_stage = big[0:P, 0:0]
        at_stage = sb("at_stage", [P, T, P])
        o2 = 2 * D

        def cut2(n):
            nonlocal o2
            o2 += n
            return hot[:, o2 - n:o2]

        topv, topf, tops, topd = (cut2(FH * TOP).rearrange("p (h k) -> p h k", h=FH) for _ in range(4))
        topi = cut2(FH * TOP).bitcast(U32).rearrange("p (h k) -> p h k", h=FH)
        negm, den, rden = (cut2(FH) for _ in range(3))

        psum = ctx.enter_context(nc.psum_tensor("psum", [128, 8 * 512], FP32))

        def bank(b, n=1):
            return psum[:, b * 512:(b + n) * 512]

        names = """edges_loaded x_loaded wv_loaded wn_loaded wc_loaded wo_loaded wf_loaded wu_loaded wd_loaded
            keys_loaded omega_loaded bias_loaded pair_loaded const_ready pool_step vec_step edges_float
            edges_transposed edge_cols_ready cand_ready candT_ready cand_max_ready cand_row_ready ranges_ready
            setup_transposed setup_stored stats_ready rstd_ready xn_ready xnT_psum x_staged xnT_stored
            v_psum beta_psum wc_psum v_stored beta_stored wc_added om_zeroed
            q_psum k_psum q_stored k_stored fq_psum ssq_psum ssk_psum fk_psum fq_min ssq_max ssk_max fk_min
            fq_exp ssq_exp ssk_exp fk_exp kphi_ready qphi_ready kv_psum kv_stored num_psum den_psum
            attn_ready mix_step wo_psum wo_added
            scratch_ready adj_done adj_stored
            gnn_psum cnt_psum at_staged x1_step xn2_ready xn2T_psum xn2T_stored q2_psum q2_stored sim_psum
            sim_stored hd_psum hd_stored hd_sq gelu_step gelu_u tanh_done gelu_ready topk_step topv_ready
            all_ready negm_ready ex1_done rest_ready topd_ready topd_exp ex2_done diff_ready sel_step
            com_ready comT_psum comT_stored out_psum out_ready out_stored var2_ready rstd2_ready passed
            """.split()
        S = {n: sem(n) for n in names}
        hot_ready = [sem(f"hot_ready{k}") for k in range(CT)]
        hot_free = [sem(f"hot_free{k}") for k in range(CT)]

        def load_range(eng, which, j):
            return eng.value_load(rng_i[0:1, which, bass.ds(j, 1)], min_val=0, max_val=T * NCH)

        block = ctx.enter_context(nc.Block())

        @block.sync
        def _(sp):
            sp.dma_start(acc[:, :, :], x.rearrange("(t p) d -> p t d", p=P)).then_inc(S["x_loaded"], 16)
            sp.dma_start(edges_i[:, 0, :], src.rearrange("(p c) -> p c", p=NCH)).then_inc(S["edges_loaded"], 16)
            sp.dma_start(edges_i[:, 1, :], dst.rearrange("(p c) -> p c", p=NCH)).then_inc(S["edges_loaded"], 16)
            for i, (w, s) in enumerate([(Wv, "wv_loaded"), (wn, "wn_loaded"), (wc, "wc_loaded"), (Wo, "wo_loaded")]):
                sp.dma_start(W[:, i], w.rearrange("(k p) d -> p k d", p=128)).then_inc(S[s], 16)
            sp.dma_start(wf_sb[:, :, :], wf.rearrange("(k p) d -> p k d", p=128)).then_inc(S["wf_loaded"], 16)
            wqv = Wq.rearrange("(k p) (c m) -> c p k m", p=128, m=128)
            wkv = Wk.rearrange("(k p) (c m) -> c p k m", p=128, m=128)
            sp.dma_start(w_pair[:, 0], wqv[0]).then_inc(S["pair_loaded"], 16)
            sp.dma_start(w_pair[:, 1], wkv[0]).then_inc(S["pair_loaded"], 16)
            with sp.Fori(1, NPAIR) as c:
                sp.wait_ge(S["k_psum"], c)
                sp.dma_start(w_pair[:, 0], wqv[bass.ds(c, 1)].rearrange("a p k m -> p (a k) m")).then_inc(S["pair_loaded"], 16)
                sp.dma_start(w_pair[:, 1], wkv[bass.ds(c, 1)].rearrange("a p k m -> p (a k) m")).then_inc(S["pair_loaded"], 16)
            outv = out.rearrange("(t p) d -> t p d", p=P)
            with sp.Fori(0, T) as t:
                sp.wait_ge(S["out_ready"], t + 2)
                sp.dma_start(outv[bass.ds(t, 1)].rearrange("a p d -> p (a d)"),
                             acc[:, bass.ds(t, 1), :].rearrange("p a d -> p (a d)")).then_inc(S["out_stored"], 16)
            sp.wait_ge(S["out_stored"], 16 * T)

        @block.gpsimd
        def _(pool):
            g = nc.gpsimd
            step = Steps(pool, S["pool_step"])
            g.memset(ident[:, :], 0.0)
            g.memset(om_qb[:, :], 0.0)
            g.memset(om_kb[:, :], 0.0).then_inc(S["om_zeroed"], 1)
            g.iota(iota[:, :], [[1, N]], base=0, channel_multiplier=0, allow_small_or_imprecise_dtypes=True)
            g.iota(blk_lo[:, :], [[P, T]], base=0, channel_multiplier=0, allow_small_or_imprecise_dtypes=True)
            g.iota(blk_hi[:, :], [[P, T]], base=P, channel_multiplier=0, allow_small_or_imprecise_dtypes=True)
            g.iota(ch_rank[:, 0:1], [[0, 1]], base=1, channel_multiplier=1, allow_small_or_imprecise_dtypes=True)
            g.iota(ch_rank[:, 1:2], [[0, 1]], base=NCH, channel_multiplier=-1, allow_small_or_imprecise_dtypes=True)
            g.memset(zrow[:, :], 0.0)
            g.memset(ones1[:, :], 1.0)
            g.memset(mhalf[:, :], -0.5)
            g.memset(kv_blk[:, :], 0.0)
            g.memset(ones_blk[:, :], 0.0)
            g.memset(pair_ones[:, :], 0.0)
            step.link(g.memset(vaug[:, :, :, VC - 1:VC], 1.0))
            g.memset(pair_ones[0:DH, 0:DH], 1.0)
            step.link(g.memset(pair_ones[DH:128, DH:128], 1.0))
            g.affine_select(out=ident[:, :], in_=ident[:, :], compare_op=ALU.not_equal, fill=1.0,
                            base=0, pattern=[[-1, 128]], channel_multiplier=1).then_inc(S["const_ready"], 1)
            pool.wait_ge(S["om_zeroed"], 1)
            for b in range(2):
                for t_, s_ in ((om_qb, om_q), (om_kb, om_k)):
                    pool.dma_start(t_[b * DH:(b + 1) * DH, b * DH:(b + 1) * DH], s_).then_inc(S["omega_loaded"], 16)
            pool.wait_ge(S["stats_ready"], 1)
            step.link(g.tensor_scalar(rstd[:, :], ag[:, :, 1], LN_EPS, None, ALU.add))
            g.tensor_tensor(rstd[:, :], rstd[:, :], mhalf[:, :], ALU.pow).then_inc(S["rstd_ready"], 1)

            def rstd2(t):
                hold(pool, S["var2_ready"], t + 1, S["passed"])
                g.tensor_scalar(rstd[:, 0:1], ag[:, 0, 1:2], LN_EPS, None, ALU.add).then_inc(S["gelu_step"], 1)
                pool.wait_ge(S["gelu_step"], 3 * t + (1 if isinstance(t, int) and t == 0 else 0))
                g.tensor_tensor(rstd[:, 0:1], rstd[:, 0:1], mhalf[:, 0:1], ALU.pow).then_inc(S["rstd2_ready"], 1)

            def gelu_in(t):
                hold(pool, S["hd_stored"], t + 2, S["passed"])
                g.tensor_scalar(hu, hu, GELU_A, 1.0, ALU.mult, ALU.add).then_inc(S["gelu_step"], 1)
                pool.wait_ge(S["gelu_step"], 3 * t + 2)
                g.tensor_tensor(hu, hu, hx, ALU.mult).then_inc(S["gelu_u"], 1)

            def gelu_out(t, last=False):
                hold(pool, S["tanh_done"], t + 1, S["passed"])
                g.tensor_scalar(hu, hu, 0.5, 0.5, ALU.mult, ALU.add).then_inc(S["gelu_step"], 1)
                pool.wait_ge(S["gelu_step"], 3 * t + (3 if last else 4))
                g.tensor_tensor(gl, hu, hx, ALU.mult).then_inc(S["gelu_ready"], 1)

            def all_scores(t):
                pool.wait_ge(S["ex1_done"], t + 1)
                for half in range(2):
                    hs = slice(half * FH // 2, (half + 1) * FH // 2)
                    shp = [P, FH // 2, TOP, TOP]
                    pool.wait_ge(S["topv_ready"], 2 * t + half + 1)
                    g.tensor_tensor(allsc[:, hs].rearrange("p h (a b) -> p h a b", a=TOP),
                                    topv[:, hs].unsqueeze(3).to_broadcast(shp),
                                    topf[:, hs].unsqueeze(2).to_broadcast(shp), ALU.add)\
                        .then_inc(S["all_ready"], 1)

            def diff(t):
                pool.wait_ge(S["ex2_done"], t + 2)
                g.tensor_tensor(ex1, ex1, ex2, ALU.subtract).then_inc(S["diff_ready"], 1)

            rstd2(0)
            with pool.Fori(0, T - 1) as t:
                gelu_in(t)
                all_scores(t)
                rstd2(t + 1)
                gelu_out(t)
                diff(t)
            gelu_in(T - 1)
            all_scores(T - 1)
            gelu_out(T - 1, last=True)
            diff(T - 1)

        @block.scalar
        def _(act):
            a = nc.scalar
            for half in range(2):
                act.dma_start(keys_nat[:, half], keys[:, half * 128:(half + 1) * 128, 0, :].rearrange("h p d -> p h d"))\
                    .then_inc(S["keys_loaded"], 16)
            act.dma_start(wd_nat, w_down[0:NE, :].rearrange("(g p) d -> p g d", g=EC)).then_inc(S["wd_loaded"], 16)
            act.dma_start(wu_sb[:, :, :], w_up[0:NE, :].rearrange("(g p) d -> p g d", g=EC)).then_inc(S["wu_loaded"], 16)
            act.dma_start(bias_bc[:, :], bias.rearrange("(a d) -> a d", a=1).to_broadcast([P, D])).then_inc(S["bias_loaded"], 16)
            act.wait_ge(S["edges_transposed"], 1)
            for s in range(2):
                a.activation(edge_cols[:, s, :].rearrange("q (p a) -> q a p", p=NCH),
                             bank(s)[0:P, 0:CT * NCH].rearrange("q (a p) -> q a p", a=CT),
                             ACT.Copy).then_inc(S["edge_cols_ready"], 1)
            act.wait_ge(S["setup_transposed"], 1)
            a.activation(keysT[:, :, :], bank(2)[:, 0:2 * NK].rearrange("p (c k) -> p c k", c=2), ACT.Copy)
            a.activation(wdT[:, :, :], bank(3, 2).rearrange("p (c k) -> p c k", c=KC), ACT.Copy)\
                .then_inc(S["setup_stored"], 1)
            with act.Fori(0, T) as t:
                act.wait_ge(S["xnT_psum"], t + 2)
                act.wait_ge(S["wc_psum"], t + 1)
                a.activation(x_stage[:, :, :], bank(0)[:, 0:KC * P].rearrange("p (k n) -> p k n", k=KC),
                             ACT.Copy).then_inc(S["x_staged"], 1)
                a.activation(xnT3[:, :, bass.ds(t * P, P)], bank(0)[:, 0:KC * P].rearrange("p (k n) -> p k n", k=KC),
                             ACT.Copy).then_inc(S["xnT_stored"], 1)
                act.wait_ge(S["v_psum"], t + 1)
                a.activation(vaug[:, bass.ds(t, 1), :, 0:2 * DH].rearrange("p a c v -> p (a c) v"),
                             bank(1)[0:P].rearrange("p (c v) -> p c v", c=NPAIR), ACT.Copy).then_inc(S["v_stored"], 1)
                act.wait_ge(S["beta_psum"], t + 1)
                a.activation(beta[0:P, bass.ds(t, 1), :].rearrange("p a d -> p (a d)"), bank(2)[0:P],
                             ACT.Copy).then_inc(S["beta_stored"], 1)
            with act.Fori(0, NPAIR) as c:
                act.wait_ge(S["q_psum"], c + 1)
                a.activation(qT, psum[:, 0:N], ACT.Copy, scale=Q_SCALE)
                a.activation(sqq, psum[:, 0:N], ACT.Square, scale=Q_SCALE).then_inc(S["q_stored"], 1)
                act.wait_ge(S["k_psum"], c + 1)
                a.activation(kT, bank(3, 3)[:, 0:N], ACT.Copy, scale=Q_SCALE)
                a.activation(sqk, bank(3, 3)[:, 0:N], ACT.Square, scale=Q_SCALE).then_inc(S["k_stored"], 1)
                act.wait_ge(S["fq_min"], c + 1)
                a.activation(qphi, qphi, ACT.Exp).then_inc(S["fq_exp"], 1)
                act.wait_ge(S["ssq_max"], c + 1)
                a.activation(sqq, sqq, ACT.Exp, scale=-0.5).then_inc(S["ssq_exp"], 1)
                act.wait_ge(S["ssk_max"], c + 1)
                a.activation(nk[:, :, :], nk[:, :, :], ACT.Exp, scale=-0.5).then_inc(S["ssk_exp"], 1)
                act.wait_ge(S["fk_min"], c + 1)
                a.activation(kphi, kphi, ACT.Exp).then_inc(S["fk_exp"], 1)
            act.wait_ge(S["attn_ready"], NPAIR + 1)
            act.wait_ge(S["wo_psum"], NPAIR * T)
            with act.Fori(0, T) as j:
                act.wait_ge(S["adj_done"], j + 1)
                a.activation(AT[:, bass.ds(j, 1), :], psum[0:P, 0:N], ACT.Copy).then_inc(S["adj_stored"], 1)

            def front_stage(t):
                act.wait_ge(S["cnt_psum"], t + 1)
                a.activation(at_stage[:, :, :], AT[:, :, bass.ds(t * P, P)], ACT.Copy).then_inc(S["at_staged"], 1)

            def front(t):
                act.wait_ge(S["xn2T_psum"], t + 2)
                a.activation(xn2T, bank(2)[:, 0:KC * P].rearrange("p (k n) -> p k n", k=KC), ACT.Copy)\
                    .then_inc(S["xn2T_stored"], 1)
                act.wait_ge(S["q2_psum"], t + 1)
                a.activation(q2T, bank(3)[:, 0:KC * P].rearrange("p (k n) -> p k n", k=KC), ACT.Copy,
                             scale=BN_SCALE).then_inc(S["q2_stored"], 1)
                act.wait_ge(S["sim_psum"], t + 1)
                a.activation(sim.rearrange("p (c b) e -> p b c e", c=2),
                             bank(4, 4)[0:P].rearrange("p (b c e) -> p b c e", b=4, c=2), ACT.Copy)\
                    .then_inc(S["sim_stored"], 1)

            def back(t):
                act.wait_ge(S["hd_psum"], t + 1)
                act.wait_ge(S["com_ready"], t + 1)
                a.activation(hx, bank(1)[0:P, 0:NE], ACT.Copy)
                a.activation(hu, bank(1)[0:P, 0:NE], ACT.Square).then_inc(S["hd_stored"], 1)
                act.wait_ge(S["gelu_u"], t + 1)
                a.activation(hu, hu, ACT.Tanh, scale=GELU_C).then_inc(S["tanh_done"], 1)

            def back2(t):
                act.wait_ge(S["negm_ready"], t + 1)
                for h in range(FH):
                    last = a.activation(ex1[:, h], allsc[:, h], ACT.Exp, bias=negm[:, h:h + 1])
                last.then_inc(S["ex1_done"], 1)
                act.wait_ge(S["topd_ready"], t + 1)
                a.activation(topd, topd, ACT.Exp).then_inc(S["topd_exp"], 1)
                act.wait_ge(S["rest_ready"], t + 1)
                for h in range(FH):
                    last = a.activation(ex2[:, h], rest[:, h], ACT.Exp, bias=negm[:, h:h + 1])
                last.then_inc(S["ex2_done"], 1)

            def back3(t):
                act.wait_ge(S["comT_psum"], t + 1)
                a.activation(comT, bank(2)[:, 0:EC * P].rearrange("p (k n) -> p k n", k=EC), ACT.Copy)\
                    .then_inc(S["comT_stored"], 1)

            for n, credit in (("hd_stored", 1), ("q2_stored", 1), ("sim_stored", 1), ("comT_stored", 2),
                              ("ex1_done", 1), ("ex2_done", 1)):
                act.sem_inc(S[n], credit)
            act.wait_ge(S["adj_stored"], T + 1)
            front_stage(0)
            front(0)
            with act.Fori(0, T - 1) as t:
                front_stage(t + 1)
                back(t)
                front(t + 1)
                back2(t)
                back3(t)
            back(T - 1)
            back2(T - 1)
            back3(T - 1)

        @block.vector
        def _(dve):
            v = nc.vector
            step = Steps(dve, S["vec_step"])
            dve.wait_ge(S["edges_loaded"], 32)
            v.tensor_copy(edges_f[:, :, :], edges_i[:, :, :]).then_inc(S["edges_float"], 1)
            dve.wait_ge(S["edges_float"], 1)
            v.tensor_reduce(ch_lim[:, 0:1], edges_f[:, 1, :], axis=AX.X, op=ALU.min)
            step.link(v.tensor_reduce(ch_lim[:, 1:2], edges_f[:, 1, :], axis=AX.X, op=ALU.max))
            dve.wait_ge(S["const_ready"], 1)
            shp = [NCH, T]
            v.tensor_tensor(touch[:, 0], blk_hi[:, :], ch_lim[:, 0:1].to_broadcast(shp), ALU.is_gt)
            step.link(v.tensor_tensor(touch[:, 1], blk_lo[:, :], ch_lim[:, 1:2].to_broadcast(shp), ALU.is_le))
            step.link(v.tensor_tensor(touch[:, 2], touch[:, 0], touch[:, 1], ALU.mult))
            v.tensor_tensor(cand[:, 0], touch[:, 2], ch_rank[:, 0:1].to_broadcast(shp), ALU.mult)
            v.tensor_tensor(cand[:, 1], touch[:, 2], ch_rank[:, 1:2].to_broadcast(shp), ALU.mult)\
                .then_inc(S["cand_ready"], 1)
            dve.wait_ge(S["x_loaded"], 16)
            for t in range(T):
                last = v.bn_stats(st[:, t, :], acc[:, t, :])
            step.link(last)
            for t in range(T):
                last = v.bn_aggr(ag[:, t, :], st[:, t, :])
            last.then_inc(S["stats_ready"], 1)
            dve.wait_ge(S["candT_ready"], 1)
            v.reduce_max(cand_max[:, :], bank(5)[0:2 * T, 0:NCH], AX.X).then_inc(S["cand_max_ready"], 1)
            dve.wait_ge(S["cand_row_ready"], 1)
            step.link(v.tensor_copy(rng[0:1, 0:2, :], bank(6)[0:1, 0:2 * T].rearrange("p (k j) -> p k j", k=2)))
            step.link(v.tensor_scalar(rng[0:1, 2, :], rng[0:1, 1, :], -1.0, float(NCH), ALU.mult, ALU.add))
            step.link(v.tensor_scalar(rng[0:1, 2, :], rng[0:1, 2, :], float(NCH - 1), None, ALU.min))
            step.link(v.tensor_scalar(rng[0:1, 3, :], rng[0:1, 2, :], 1.0, None, ALU.add))
            step.link(v.tensor_tensor(rng[0:1, 3, :], rng[0:1, 3, :], rng[0:1, 0, :], ALU.max))
            step.link(v.tensor_tensor(rng[0:1, 4, :], rng[0:1, 3, :], rng[0:1, 2, :], ALU.subtract))
            step.link(v.tensor_tensor_scan(rng[0:1, 5, :], rng[0:1, 4, :], rng[0:1, 4, :], 0.0, ALU.add, ALU.max))
            step.link(v.tensor_tensor(rng[0:1, 6, :], rng[0:1, 5, :], rng[0:1, 4, :], ALU.subtract))
            v.tensor_copy(rng_i[0:1, 0, :], rng[0:1, 6, :])
            v.tensor_copy(rng_i[0:1, 1, :], rng[0:1, 5, :])
            v.tensor_copy(rng_i[0:1, 2, :], rng[0:1, 2, :]).then_inc(S["ranges_ready"], 1)

            dve.wait_ge(S["rstd_ready"], 1)
            dve.wait_ge(S["bias_loaded"], 16)
            dve.sem_inc(S["wc_added"], 1)
            with dve.Fori(0, T) as t:
                at = acc[:, bass.ds(t, 1), :].rearrange("p a d -> p (a d)")
                dve.wait_ge(S["xnT_psum"], t + 1)
                dve.wait_ge(S["wc_added"], t + 1)
                v.tensor_scalar(xn_tile, at, ag[:, bass.ds(t, 1), 0], rstd[:, bass.ds(t, 1)],
                                ALU.subtract, ALU.mult).then_inc(S["xn_ready"], 1)
                v.tensor_tensor(xa_tile, at, bias_bc[:, :], ALU.add).then_inc(S["mix_step"], 1)
                dve.wait_ge(S["mix_step"], t + 1)
                dve.wait_ge(S["wc_psum"], t + 2)
                v.tensor_tensor(at, xa_tile, bank(3)[0:P], ALU.add).then_inc(S["wc_added"], 1)

            MS = 2
            with dve.Fori(0, NPAIR) as c:
                m = Steps(dve, S["mix_step"], T + MS * c)
                dve.wait_ge(S["fq_psum"], c + 1)
                v.tensor_scalar(qphi, psum[:, 0:N], CLAMP, None, ALU.min).then_inc(S["fq_min"], 1)
                dve.wait_ge(S["ssq_psum"], c + 1)
                v.tensor_scalar(sqq, bank(3, 3)[:, 0:N], EPS * EPS, None, ALU.max).then_inc(S["ssq_max"], 1)
                dve.wait_ge(S["ssk_psum"], c + 1)
                v.tensor_scalar(nk[:, :, :], bank(6)[0:P, 0:2 * T].rearrange("p (t h) -> p t h", h=2), EPS * EPS,
                                None, ALU.max).then_inc(S["ssk_max"], 1)
                dve.wait_ge(S["fk_psum"], c + 1)
                v.tensor_scalar(kphi, psum[0:P, 0:T * 128].rearrange("p (t m) -> p t m", t=T), CLAMP, None,
                                ALU.min).then_inc(S["fk_min"], 1)
                dve.wait_ge(S["ssk_exp"], c + 1)
                m.link(v.tensor_scalar(nk[:, :, :], nk[:, :, :], EPS, None, ALU.max))
                dve.wait_ge(S["fk_exp"], c + 1)
                v.tensor_tensor(kphi.rearrange("p t (h m) -> p t h m", h=2),
                                kphi.rearrange("p t (h m) -> p t h m", h=2),
                                nk[:, :, :].unsqueeze(3).to_broadcast([P, T, 2, DH]), ALU.mult)\
                    .then_inc(S["kphi_ready"], 1)
                dve.wait_ge(S["ssq_exp"], c + 1)
                dve.wait_ge(S["fq_exp"], c + 1)
                v.scalar_tensor_tensor(qphi, sqq, EPS, qphi, ALU.max, ALU.mult).then_inc(S["qphi_ready"], 1)
                dve.wait_ge(S["kv_psum"], c + 1)
                kv = bank(7)
                v.tensor_copy(kv_blk[0:DH, 0:DH], kv[0:DH, 0:DH])
                v.tensor_copy(kv_blk[DH:128, DH:128], kv[DH:128, DH:2 * DH])
                v.tensor_copy(ones_blk[0:DH, 0:DH], kv[0:DH, VC - 1:VC].to_broadcast([DH, DH]))
                v.tensor_copy(ones_blk[DH:128, DH:128], kv[DH:128, VC - 1:VC].to_broadcast([DH, DH]))\
                    .then_inc(S["kv_stored"], 1)
                dve.wait_ge(S["den_psum"], c + 1)
                m.link(v.reciprocal(sqk, bank(3, 3)[:, 0:N]))
                v.tensor_tensor(qT, psum[:, 0:N], sqk, ALU.mult).then_inc(S["attn_ready"], 1)
                dve.wait_ge(S["wo_added"], c * T + 1)
                for t in range(T):
                    dve.wait_ge(S["wo_psum"], c * T + t + 1)
                    ins = v.tensor_tensor(acc[:, t, :], acc[:, t, :], bank(6 + t % 2)[0:P], ALU.add)
                    ins.then_inc(S["wo_added"], 1)
                assert m.n == MS

            dve.wait_ge(S["ranges_ready"], 1)
            dve.wait_ge(S["edge_cols_ready"], 2)
            dve.sem_inc(S["scratch_ready"], 1)
            for k in range(CT):
                dve.sem_inc(hot_ready[k], 1)
            with dve.Fori(0, T) as j:
                lo = load_range(dve, 0, j)
                hi = load_range(dve, 1, j)
                ch0 = load_range(dve, 2, j)
                dve.wait_ge(hot_ready[CT - 1], lo + 1)
                v.tensor_copy(iota_blk[:, :], iota[:, bass.ds(j * P, P)]).then_inc(S["scratch_ready"], 1)
                with dve.Fori(lo, hi) as slot:
                    e0 = nc.s_assert_within((slot - lo + ch0) * CT, 0, (NCH - 1) * CT,
                                            skip_runtime_bounds_check_because="the ranges are clamped to the chunks")
                    turn = dve.snap(slot + 1)
                    prep = dve.snap(slot + j + 3)
                    dve.wait_ge(hot_ready[CT - 1], turn)
                    v.tensor_copy(scr_edge[:, :, :], edge_cols[:, :, bass.ds(e0, CT)]).then_inc(S["scratch_ready"], 1)
                    dve.wait_ge(S["scratch_ready"], prep)
                    for k in range(CT):
                        dve.wait_ge(hot_free[k], turn)
                        v.tensor_scalar(hot_dst[:, k, :], iota_blk[:, :], scr_edge[:, 1, k:k + 1], None, ALU.is_equal)
                        v.tensor_scalar(hot_src[:, k, :], iota[:, :], scr_edge[:, 0, k:k + 1], None,
                                        ALU.is_equal).then_inc(hot_ready[k], 1)

            XS = 3
            KS = 10

            def residual(t):
                at = acc[:, bass.ds(t, 1), :].rearrange("p a d -> p (a d)")
                xs = Steps(dve, S["x1_step"], XS * t, S["passed"])
                hold(dve, S["cnt_psum"], t + 2, S["passed"])
                xs.link(v.reciprocal(rcnt[:, :], bank(2)[0:P, 504:505]))
                xs.link(v.scalar_tensor_tensor(at, bank(1)[0:P], rcnt[:, :], at, ALU.mult, ALU.add))
                xs.link(v.bn_stats(st[:, 0, :], at))
                v.bn_aggr(ag[:, 0, :], st[:, 0, :]).then_inc(S["var2_ready"], 1)
                assert xs.n == XS
                dve.wait_ge(S["xn2T_psum"], t + 1)
                dve.wait_ge(S["rstd2_ready"], t + 1)
                v.tensor_scalar(xn_tile, at, ag[:, 0, 0:1], rstd[:, 0:1], ALU.subtract, ALU.mult)\
                    .then_inc(S["xn2_ready"], 1)

            def heads_half(half):
                return range(half * FH // 2, (half + 1) * FH // 2)

            def top_keys(t):
                hold(dve, S["sim_stored"], t + 2, S["passed"])
                ks = Steps(dve, S["topk_step"], KS * t, S["passed"])
                for half in range(2):
                    hs = heads_half(half)
                    for h in hs:
                        last = v.max(topv[:, h, 0:8], sim[:, h])
                    ks.link(last)
                    for h in hs:
                        last = v.max_index(topi[:, h, 0:8], topv[:, h, 0:8], sim[:, h])
                    ks.link(last)
                    for h in hs:
                        last = v.match_replace(sim[:, h], topv[:, h, 0:8], sim[:, h], LOWEST)
                    ks.link(last)
                    for h in hs:
                        last = v.max(topv[:, h, 8:16], sim[:, h])
                    ks.link(last)
                    for h in hs:
                        last = v.max_index(topi[:, h, 8:16], topv[:, h, 8:16], sim[:, h])
                    ks.link(last)
                    v.tensor_copy(topf[:, hs[0]:hs[-1] + 1], topi[:, hs[0]:hs[-1] + 1]).then_inc(S["topv_ready"], 1)
                assert ks.n == KS

            SS = 3 + 2 + 8

            def top_scores(t):
                ss = Steps(dve, S["sel_step"], SS * t, S["passed"])
                for half in range(2):
                    hold(dve, S["all_ready"], 2 * t + half + 1, S["passed"])
                    for h in heads_half(half):
                        last = v.max(tops[:, h, 0:8], allsc[:, h])
                ss.link(last)
                v.tensor_scalar(negm, tops[:, :, 0], -1.0, None, ALU.mult).then_inc(S["negm_ready"], 1)
                hold(dve, S["ex2_done"], t + 1, S["passed"])
                for h in range(FH):
                    last = v.match_replace(rest[:, h], tops[:, h, 0:8], allsc[:, h], LOWEST)
                ss.link(last)
                for h in range(FH):
                    last = v.max(tops[:, h, 8:16], rest[:, h])
                ss.link(last)
                for h in range(FH):
                    last = v.match_replace(rest[:, h], tops[:, h, 8:16], rest[:, h], LOWEST)
                last.then_inc(S["rest_ready"], 1)
                v.tensor_tensor(topd, tops, negm.unsqueeze(2).to_broadcast([P, FH, TOP]), ALU.add)\
                    .then_inc(S["topd_ready"], 1)
                dve.wait_ge(S["topd_exp"], t + 1)
                ss.link(v.reduce_sum(den, topd, AX.X))
                ss.link(v.reciprocal(rden, den))
                hold(dve, S["diff_ready"], t + 1, S["passed"])
                ss.link(v.tensor_scalar(sel, ex1[:, 0], rden[:, 0:1], None, ALU.mult))
                for h in range(1, FH):
                    ss.link(v.scalar_tensor_tensor(sel, ex1[:, h], rden[:, h:h + 1], sel, ALU.mult, ALU.add))
                assert ss.n == SS, ss.n
                dve.wait_ge(S["gelu_ready"], t + 1)
                v.tensor_tensor(com, sel, gl, ALU.mult).then_inc(S["com_ready"], 1)

            def add_out(t):
                at = acc[:, bass.ds(t, 1), :].rearrange("p a d -> p (a d)")
                dve.wait_ge(S["out_psum"], t + 1)
                v.tensor_tensor(at, at, bank(0)[0:P], ALU.add).then_inc(S["out_ready"], 1)

            dve.sem_inc(S["com_ready"], 1)
            dve.sem_inc(S["out_ready"], 1)
            residual(0)
            top_keys(0)
            residual(1)
            top_scores(0)
            with dve.Fori(1, T - 1) as t:
                top_keys(t)
                add_out(t - 1)
                residual(t + 1)
                top_scores(t)
            top_keys(T - 1)
            add_out(T - 2)
            top_scores(T - 1)
            add_out(T - 1)

        @block.tensor
        def _(pe):
            te = nc.tensor
            pe.wait_ge(S["const_ready"], 1)
            pe.wait_ge(S["edges_float"], 1)
            for s in range(2):
                for k in range(CT):
                    last = te.transpose(bank(s)[0:P, k * NCH:(k + 1) * NCH], edges_f[:, s, k * P:(k + 1) * P],
                                        ident[0:NCH, 0:NCH])
            last.then_inc(S["edges_transposed"], 1)
            pe.wait_ge(S["cand_ready"], 1)
            te.transpose(bank(5)[0:2 * T, 0:NCH], cand[:, :, :].rearrange("p k j -> p (k j)"),
                         ident[0:NCH, 0:NCH]).then_inc(S["candT_ready"], 1)
            pe.wait_ge(S["cand_max_ready"], 1)
            te.transpose(bank(6)[0:1, 0:2 * T], cand_max[:, :], ident[0:2 * T, 0:2 * T])\
                .then_inc(S["cand_row_ready"], 1)
            pe.wait_ge(S["keys_loaded"], 32)
            for c in range(2):
                for gk in range(2):
                    te.transpose(bank(2)[:, c * NK + gk * 128:c * NK + (gk + 1) * 128],
                                 keys_nat[:, gk, 4 * c:4 * c + 4, :].rearrange("p h d -> p (h d)"), ident[:, :])
            pe.wait_ge(S["wd_loaded"], 16)
            for c in range(KC):
                for gk in range(EC):
                    last = te.transpose(bank(3, 2)[:, c * NE + gk * 128:c * NE + (gk + 1) * 128],
                                        wd_nat[:, gk, c * 128:(c + 1) * 128], ident[:, :])
            last.then_inc(S["setup_transposed"], 1)
            pe.wait_ge(S["setup_stored"], 1)
            pe.wait_ge(S["edge_cols_ready"], 2)
            pe.wait_ge(S["wv_loaded"], 16)
            pe.wait_ge(S["wn_loaded"], 16)
            pe.wait_ge(S["wc_loaded"], 16)
            for s in ("xnT_psum", "wc_psum", "v_stored", "beta_stored", "xnT_stored"):
                pe.sem_inc(S[s], 1)
            with pe.Fori(0, T) as t:
                pe.wait_ge(S["xn_ready"], t + 1)
                pe.wait_ge(S["xnT_stored"], t + 1)
                for k in range(KC):
                    last = te.transpose(bank(0)[:, k * P:(k + 1) * P], xn_tile[:, k * 128:(k + 1) * 128],
                                        ident[0:P, 0:P])
                last.then_inc(S["xnT_psum"], 1)
                pe.wait_ge(S["x_staged"], t + 1)
                for b, w, s, free in ((1, Wv_sb, "v_psum", "v_stored"), (2, wn_sb, "beta_psum", "beta_stored"),
                                      (3, wc_sb, "wc_psum", "wc_added")):
                    pe.wait_ge(S[free], t + 1)
                    for k in range(KC):
                        last = te.matmul(bank(b)[0:P], x_stage[:, k, :], w[:, k, :], start=(k == 0), stop=(k == KC - 1))
                    last.then_inc(S[s], 1)

            pe.wait_ge(S["xnT_stored"], T + 1)
            pe.wait_ge(S["v_stored"], T + 1)
            pe.wait_ge(S["wc_added"], T + 1)
            pe.wait_ge(S["beta_stored"], T + 1)
            pe.wait_ge(S["omega_loaded"], 64)
            pe.wait_ge(S["wo_loaded"], 16)
            pe.sem_inc(S["attn_ready"], 1)
            pe.sem_inc(S["wo_added"], 1)
            with pe.Fori(0, NPAIR) as c:
                pe.wait_ge(S["pair_loaded"], c * 32 + 32)
                pe.wait_ge(S["attn_ready"], c + 1)
                for i, s in enumerate(("q_psum", "k_psum")):
                    for lo_, hi_ in banks:
                        for k in range(KC):
                            last = te.matmul(bank(3 * i, 3)[:, lo_:hi_], w_pair[:, i, k, :], xnT3[:, k, lo_:hi_],
                                             start=(k == 0), stop=(k == KC - 1))
                    last.then_inc(S[s], 1)
                pe.wait_ge(S["q_stored"], c + 1)
                for lo_, hi_ in banks:
                    last = te.matmul(psum[:, lo_:hi_], om_qb[:, :], qT[:, lo_:hi_], start=True, stop=True)
                last.then_inc(S["fq_psum"], 1)
                pe.wait_ge(S["k_stored"], c + 1)
                for lo_, hi_ in banks:
                    last = te.matmul(bank(3, 3)[:, lo_:hi_], pair_ones[:, :], sqq[:, lo_:hi_], start=True, stop=True)
                last.then_inc(S["ssq_psum"], 1)
                pe.wait_ge(S["wo_added"], c * T + 1)
                for t in range(T):
                    last = te.matmul(bank(6)[0:P, 2 * t:2 * t + 2], sqk[:, t * P:(t + 1) * P],
                                     pair_ones[:, DH - 1:DH + 1], start=True, stop=True)
                last.then_inc(S["ssk_psum"], 1)
                pe.wait_ge(S["fq_min"], c + 1)
                for t in range(T):
                    last = te.matmul(psum[0:P, t * 128:(t + 1) * 128], kT[:, t * P:(t + 1) * P], om_kb[:, :],
                                     start=True, stop=True)
                last.then_inc(S["fk_psum"], 1)
                pe.wait_ge(S["kphi_ready"], c + 1)
                for t in range(T):
                    last = te.matmul(bank(7)[:, 0:VC], kphi[:, t, :],
                                     vaug[:, t, bass.ds(c, 1), :].rearrange("p a v -> p (a v)"),
                                     start=(t == 0), stop=(t == T - 1))
                last.then_inc(S["kv_psum"], 1)
                pe.wait_ge(S["kv_stored"], c + 1)
                pe.wait_ge(S["qphi_ready"], c + 1)
                for lo_, hi_ in banks:
                    te.matmul(psum[:, lo_:hi_], kv_blk[:, :], qphi[:, lo_:hi_], start=True, stop=True)
                for lo_, hi_ in banks:
                    last = te.matmul(bank(3, 3)[:, lo_:hi_], ones_blk[:, :], qphi[:, lo_:hi_], start=True, stop=True)
                last.then_inc(S["den_psum"], 1)
                pe.wait_ge(S["attn_ready"], c + 2)
                for t in range(T):
                    if t >= 2:
                        pe.wait_ge(S["wo_added"], c * T + t)
                    te.matmul(bank(6 + t % 2)[0:P], qT[:, t * P:(t + 1) * P],
                              Wo_sb[:, bass.ds(c, 1), :].rearrange("p a d -> p (a d)"),
                              start=True, stop=True).then_inc(S["wo_psum"], 1)

            pe.wait_ge(S["ranges_ready"], 1)
            for k in range(CT):
                pe.sem_inc(hot_free[k], 1)
            pe.sem_inc(S["adj_stored"], 1)
            with pe.Fori(0, T) as j:
                lo = load_range(pe, 0, j)
                hi = load_range(pe, 1, j)
                pe.wait_ge(S["adj_stored"], j + 1)
                for lo_, hi_ in banks:
                    te.matmul(psum[0:P, lo_:hi_], zrow[0:1, 0:P], zrow[0:1, 0:hi_ - lo_], start=True, stop=False)
                with pe.Fori(lo, hi) as slot:
                    for k in range(CT):
                        pe.wait_ge(hot_ready[k], slot + 2)
                        for lo_, hi_ in banks:
                            last = te.matmul(psum[0:P, lo_:hi_], hot_dst[:, k, :], hot_src[:, k, lo_:hi_],
                                             start=False, stop=False)
                        last.then_inc(hot_free[k], 1)
                for lo_, hi_ in banks:
                    last = te.matmul(psum[0:P, lo_:hi_], zrow[0:1, 0:P], zrow[0:1, 0:hi_ - lo_], start=False, stop=True)
                last.then_inc(S["adj_done"], 1)

            def gnn(t):
                pe.wait_ge(S["at_staged"], t + 1)
                pe.wait_ge(S["hd_stored"], t + 1)
                for j in range(T):
                    last = te.matmul(bank(1)[0:P], at_stage[:, j, :], beta[0:P, j, :], start=(j == 0), stop=(j == T - 1))
                for j in range(T):
                    last = te.matmul(bank(2)[0:P, 504:505], at_stage[:, j, :], ones1[:, 0:1],
                                     start=(j == 0), stop=(j == T - 1))
                last.then_inc(S["cnt_psum"], 1)

            def front(t):
                pe.wait_ge(S["xn2_ready"], t + 1)
                pe.wait_ge(S["comT_stored"], t + 1)
                for k in range(KC):
                    last = te.transpose(bank(2)[:, k * P:(k + 1) * P], xn_tile[:, k * 128:(k + 1) * 128],
                                        ident[0:P, 0:P])
                last.then_inc(S["xn2T_psum"], 1)
                pe.wait_ge(S["xn2T_stored"], t + 1)
                pe.wait_ge(S["q2_stored"], t + 1)
                for m in range(KC):
                    for k in range(KC):
                        last = te.matmul(bank(3)[:, m * P:(m + 1) * P], wf_sb[:, k, m * 128:(m + 1) * 128],
                                         xn2T[:, k, :], start=(k == 0), stop=(k == KC - 1))
                last.then_inc(S["q2_psum"], 1)
                pe.wait_ge(S["q2_stored"], t + 2)
                pe.wait_ge(S["sim_stored"], t + 1)
                for h in range(FH):
                    c, b = h // 4, h % 4
                    last = te.matmul(bank(4 + b)[0:P, c * NK:(c + 1) * NK], q2T[b * DK:(b + 1) * DK, c, :],
                                     keysT[b * DK:(b + 1) * DK, c, :], start=True, stop=True)
                last.then_inc(S["sim_psum"], 1)
                for k in range(KC):
                    last = te.matmul(bank(1)[0:P, 0:NE], q2T[:, k, :], wdT[:, k, :], start=(k == 0), stop=(k == KC - 1))
                last.then_inc(S["hd_psum"], 1)

            def combine(t):
                pe.wait_ge(S["com_ready"], t + 2)
                for k in range(EC):
                    last = te.transpose(bank(2)[:, k * P:(k + 1) * P], com[:, k * 128:(k + 1) * 128], ident[0:P, 0:P])
                last.then_inc(S["comT_psum"], 1)
                pe.wait_ge(S["comT_stored"], t + 3)
                pe.wait_ge(S["out_ready"], t + 1)
                for k in range(EC):
                    last = te.matmul(bank(0)[0:P], comT[:, k, :], wu_sb[:, k, :], start=(k == 0), stop=(k == EC - 1))
                last.then_inc(S["out_psum"], 1)

            pe.wait_ge(S["adj_stored"], T + 1)
            pe.wait_ge(S["wf_loaded"], 16)
            pe.wait_ge(S["wu_loaded"], 16)
            pe.sem_inc(S["cnt_psum"], 1)
            pe.sem_inc(S["xn2T_psum"], 1)
            gnn(0)
            front(0)
            with pe.Fori(0, T - 1) as t:
                gnn(t + 1)
                front(t + 1)
                combine(t)
            combine(T - 1)


_INS = ["x", "src", "dst", "L0_gnn_wc", "L0_gnn_wn", "L0_gnn_bias", "L0_mix_Wq", "L0_mix_Wk", "L0_mix_Wv", "L0_mix_Wo",
        "L0_mix_omega_q", "L0_mix_omega_k", "L0_ffn_w_q", "L0_ffn_keys", "L0_ffn_weight_down_embed",
        "L0_ffn_weight_up_embed"]


def kernel(**inputs):
    import numpy as _np
    import concourse.bacc as _bacc
    from concourse import mybir as _mybir
    from concourse.bass_utils import run_bass_kernel_spmd as _run

    nc = _bacc.Bacc("TRN2", target_bir_lowering=False, num_devices=1)
    arrays, args = {}, []
    for name in _INS:
        a = _np.ascontiguousarray(inputs[name])
        arrays[f"in_{name}_dram"] = a
        args.append(nc.dram_tensor(f"in_{name}_dram", a.shape, _mybir.dt.from_np(a.dtype), kind="ExternalInput").ap())
    shape = inputs["x"].shape
    out = nc.dram_tensor("out_dram", shape, _mybir.dt.float32, kind="ExternalOutput").ap()
    gps_layer(nc, *args, out)
    r = _run(nc, [arrays], core_ids=[0])
    return r.results[0]["out_dram"]
```

```python
import concourse.bass as bass
from concourse import mybir
from contextlib import ExitStack

FP32 = mybir.dt.float32
FP16 = mybir.dt.float16
I32 = mybir.dt.int32
U32 = mybir.dt.uint32
U16 = mybir.dt.uint16
ALU = mybir.AluOpType
ACT = mybir.ActivationFunctionType
AX = mybir.AxisListType


def hold(eng, sem, value, passed):
    eng.wait_ge(sem, value)
    eng.sem_inc(passed, 1)


class Steps:

    def __init__(self, eng, sem, base=0, passed=None):
        self.eng, self.sem, self.base, self.n, self.passed = eng, sem, base, 0, passed

    def link(self, ins):
        self.n += 1
        ins.then_inc(self.sem, 1)
        if self.passed is None:
            self.eng.wait_ge(self.sem, self.base + self.n)
        else:
            hold(self.eng, self.sem, self.base + self.n, self.passed)


def gps_layer(nc, x, src, dst, wc, wn, bias, Wq, Wk, Wv, Wo, om_q, om_k, wf, keys, w_down, w_up, out):
    N, D = x.shape
    E = src.shape[0]
    P = 125
    T = N // P
    KC = D // 128
    H = 8
    DH = D // H
    NPAIR = H // 2
    VC = 2 * DH + 1
    CT = 4
    NCH = E // P // CT
    FH = keys.shape[0]
    NK = keys.shape[1]
    DK = keys.shape[3]
    TOP = 16
    NE = TOP * TOP
    EC = NE // 128
    Q_SCALE = 1.0 / DH ** 0.5
    BN_SCALE = 1.0 / (1.0 + 1e-5) ** 0.5
    LN_EPS = 1e-5
    EPS = 1e-8
    CLAMP = 50.0
    LOWEST = -3.0e38
    GELU_C = 0.7978845608028654
    GELU_A = 0.044715
    banks = [(0, 512), (512, 1024), (1024, N)]

    ctx = ExitStack()
    with ctx:
        def sb(name, shape, dt=FP32):
            return ctx.enter_context(nc.sbuf_tensor(name, shape, dt))

        def sem(name):
            return ctx.enter_context(nc.semaphore(name))

        ident = sb("ident", [128, 128])
        pair_ones = sb("pair_ones", [128, 128])
        iota = sb("iota", [P, N], FP16)
        zrow = sb("zrow", [1, 512], FP16)
        om_qb = sb("om_qb", [128, 128])
        om_kb = sb("om_kb", [128, 128])
        acc = sb("acc", [P, T, D])
        beta = sb("beta", [128, T, D])
        W = sb("W", [128, 4, KC, D])
        wf_sb = sb("wf_sb", [128, KC, D])
        wu_sb = sb("wu_sb", [128, EC, D])
        wdT = sb("wdT", [128, KC, NE])
        keysT = sb("keysT", [128, 2, NK])
        bias_bc = sb("bias_bc", [P, D])
        xnT = sb("xnT", [128, KC * N])
        adj = sb("adj", [P, T, N], U16)
        vaug = sb("vaug", [P, T, NPAIR, VC])
        work = sb("work", [128, 5 * N + 2 * CT * P // 2])
        col_sum = sb("col_sum", [P, N])
        w_pair = sb("w_pair", [128, 2, KC, 128])
        x_stage = sb("x_stage", [128, KC, P])
        kv_blk = sb("kv_blk", [128, 128])
        ones_blk = sb("ones_blk", [128, 128])
        edge_cols = sb("edge_cols", [P, 2, NCH * CT])
        ch_lim = sb("ch_lim", [NCH, 2])
        ch_rank = sb("ch_rank", [NCH, 2])
        blk_lo = sb("blk_lo", [NCH, T])
        blk_hi = sb("blk_hi", [NCH, T])
        touch = sb("touch", [NCH, 3, T])
        cand = sb("cand", [NCH, 2, T])
        cand_max = sb("cand_max", [2 * T, 1])
        rng = sb("rng", [1, 8, T])
        rng_i = sb("rng_i", [1, 3, T], I32)
        st = sb("st", [P, T, 6])
        ag = sb("ag", [P, T, 2])
        rstd = sb("rstd", [P, T])
        mhalf = sb("mhalf", [P, T])
        nk = sb("nk", [P, T, 2])
        rcnt = sb("rcnt", [P, T])
        ones1 = sb("ones1", [P, 2])

        xnT3 = xnT[:, 0:KC * N].rearrange("p (k n) -> p k n", k=KC)
        Wv_sb, wn_sb, wc_sb, Wo_sb = (W[:, i] for i in range(4))
        qT, kT, sqq = (work[:, i * N:(i + 1) * N] for i in range(3))
        W_used = W[:, 0:3].rearrange("p a k d -> p (a k d)")
        qphi, num, den_all = (W_used[:, i * N:(i + 1) * N] for i in range(3))
        sqk = work[:, 3 * N:4 * N]
        kphi = work[0:P, 4 * N:4 * N + T * 128].rearrange("p (t m) -> p t m", t=T)
        edges_i = kT[0:NCH, 0:2 * CT * P].bitcast(I32).rearrange("p (s e) -> p s e", s=2)
        edges_f = sqq[0:NCH, 0:2 * CT * P].rearrange("p (s e) -> p s e", s=2)
        at_stage = kT[0:P, :].rearrange("p (j s) -> p j s", j=T)
        hot_src = work[0:P, N:5 * N].bitcast(FP16).rearrange("p (k n) -> p k n", k=2 * CT)
        hot_dst = work[0:P, 5 * N:5 * N + CT * P].bitcast(FP16).rearrange("p (k n) -> p k n", k=2 * CT)
        xn_tile = qT[0:P, 0:D]
        wd_nat = beta[:, 0:EC, :]
        keys_nat = beta[:, EC, :].rearrange("p (g h d) -> p g h d", g=2, h=FH)
        ffn = W[:, 0:4].rearrange("p a k d -> p (a k d)")
        sim, allsc, rest, ex1 = (ffn[0:P, i * FH * NK:(i + 1) * FH * NK].rearrange("p (h e) -> p h e", h=FH)
                                 for i in range(4))
        ex2 = xnT[0:P, 0:FH * NK].rearrange("p (h e) -> p h e", h=FH)
        o = FH * NK

        def cut(n, rows=128):
            nonlocal o
            o += n
            return xnT[0:rows, o - n:o]

        xn2T = cut(KC * P).rearrange("p (k n) -> p k n", k=KC)
        q2T = cut(KC * P).rearrange("p (k n) -> p k n", k=KC)
        comT = cut(EC * P).rearrange("p (k n) -> p k n", k=EC)
        hx, hu = (cut(EC * P) for _ in range(2))
        gl = cut(2 * EC * P).rearrange("p (g n) -> p g n", g=2)
        o2 = 0

        def cut2(n):
            nonlocal o2
            o2 += n
            return work[0:P, 3 * N + o2 - n:3 * N + o2]

        topv, topf, tops, topd = (cut2(FH * TOP).rearrange("p (h k) -> p h k", h=FH) for _ in range(4))
        topi = cut2(FH * TOP).bitcast(U32).rearrange("p (h k) -> p h k", h=FH)
        negm, den, rden = (cut2(FH) for _ in range(3))

        psum = ctx.enter_context(nc.psum_tensor("psum", [128, 8 * 512], FP32))

        def bank(b, n=1):
            return psum[:, b * 512:(b + n) * 512]

        def bank67(j):
            return psum[0:P, bass.ds(6 * 512 + (j % 2) * 512, 512)]

        def tile_of(t):
            return acc[:, bass.ds(t, 1), :].rearrange("p a d -> p (a d)")

        names = """st_psum w_ready den_ready score_step edges_loaded x_loaded wv_loaded wn_loaded wc_loaded wo_loaded wf_loaded wu_loaded wd_loaded
            keys_loaded omega_loaded bias_loaded pair_loaded const_ready pool_step vec_step edges_float
            edges_transposed edge_cols_ready cand_ready candT_ready cand_max_ready cand_row_ready ranges_ready
            setup_transposed setup_stored stats_ready rstd_ready xn_ready xnT_psum x_staged xnT_stored
            v_psum beta_psum wc_psum v_stored beta_stored wc_added om_zeroed
            q_psum k_psum q_stored k_stored fq_psum ssq_psum ssk_psum fk_psum fq_min ssq_max ssk_max fk_min
            fq_exp ssq_exp ssk_exp fk_exp kphi_ready qphi_ready kv_psum kv_stored den_psum num_stored
            attn_ready den_inv mix_step wo_psum wo_added
            adj_done adj_stored col_summed count_psum count_inv
            gnn_psum at_staged x1_step xn2_ready xn2T_psum xn2T_stored q2_psum q2_stored sim_psum
            sim_stored hd_psum hd_stored hd_sq gelu_step gelu_u tanh_done gelu_ready topk_step topv_ready
            all_ready negm_ready ex1_done rest_ready topd_ready topd_exp ex2_done diff_ready sel_step
            com_ready comT_psum comT_stored out_psum out_ready out_stored var2_ready rstd2_ready passed
            """.split()
        S = {n: sem(n) for n in names}
        hot_ready = [sem(f"hot_ready{k}") for k in range(CT)]
        hot_free = [sem(f"hot_free{k}") for k in range(CT)]

        def load_range(eng, which, j):
            return eng.value_load(rng_i[0:1, which, bass.ds(j, 1)], min_val=0, max_val=T * NCH)

        block = ctx.enter_context(nc.Block())

        @block.sync
        def _(sp):
            sp.dma_start(acc[:, :, :], x.rearrange("(t p) d -> p t d", p=P)).then_inc(S["x_loaded"], 16)
            sp.dma_start(edges_i[:, 0, :], src.rearrange("(p c) -> p c", p=NCH)).then_inc(S["edges_loaded"], 16)
            sp.dma_start(edges_i[:, 1, :], dst.rearrange("(p c) -> p c", p=NCH)).then_inc(S["edges_loaded"], 16)
            for i, (w, s) in enumerate([(Wv, "wv_loaded"), (wn, "wn_loaded"), (wc, "wc_loaded"), (Wo, "wo_loaded")]):
                sp.dma_start(W[:, i], w.rearrange("(k p) d -> p k d", p=128)).then_inc(S[s], 16)
            sp.dma_start(wf_sb[:, :, :], wf.rearrange("(k p) d -> p k d", p=128)).then_inc(S["wf_loaded"], 16)
            wqv = Wq.rearrange("(k p) (c m) -> c p k m", p=128, m=128)
            wkv = Wk.rearrange("(k p) (c m) -> c p k m", p=128, m=128)
            sp.dma_start(w_pair[:, 0], wqv[0]).then_inc(S["pair_loaded"], 16)
            sp.dma_start(w_pair[:, 1], wkv[0]).then_inc(S["pair_loaded"], 16)
            with sp.Fori(1, NPAIR) as c:
                sp.wait_ge(S["k_psum"], c)
                sp.dma_start(w_pair[:, 0], wqv[bass.ds(c, 1)].rearrange("a p k m -> p (a k) m")).then_inc(S["pair_loaded"], 16)
                sp.dma_start(w_pair[:, 1], wkv[bass.ds(c, 1)].rearrange("a p k m -> p (a k) m")).then_inc(S["pair_loaded"], 16)
            outv = out.rearrange("(t p) d -> t p d", p=P)
            with sp.Fori(0, T) as t:
                sp.wait_ge(S["out_ready"], t + 2)
                sp.dma_start(outv[bass.ds(t, 1)].rearrange("a p d -> p (a d)"),
                             acc[:, bass.ds(t, 1), :].rearrange("p a d -> p (a d)")).then_inc(S["out_stored"], 16)
            sp.wait_ge(S["out_stored"], 16 * T)

        @block.gpsimd
        def _(pool):
            g = nc.gpsimd
            step = Steps(pool, S["pool_step"])
            g.memset(ident[:, :], 0.0)
            g.memset(om_qb[:, :], 0.0)
            g.memset(om_kb[:, :], 0.0).then_inc(S["om_zeroed"], 1)
            g.iota(iota[:, :], [[1, N]], base=0, channel_multiplier=0, allow_small_or_imprecise_dtypes=True)
            g.iota(blk_lo[:, :], [[P, T]], base=0, channel_multiplier=0, allow_small_or_imprecise_dtypes=True)
            g.iota(blk_hi[:, :], [[P, T]], base=P, channel_multiplier=0, allow_small_or_imprecise_dtypes=True)
            g.iota(ch_rank[:, 0:1], [[0, 1]], base=1, channel_multiplier=1, allow_small_or_imprecise_dtypes=True)
            g.iota(ch_rank[:, 1:2], [[0, 1]], base=NCH, channel_multiplier=-1, allow_small_or_imprecise_dtypes=True)
            g.memset(zrow[:, :], 0.0)
            g.memset(ones1[:, :], 1.0)
            g.memset(mhalf[:, :], -0.5)
            g.memset(kv_blk[:, :], 0.0)
            g.memset(ones_blk[:, :], 0.0)
            g.memset(pair_ones[:, :], 0.0)
            step.link(g.memset(vaug[:, :, :, VC - 1:VC], 1.0))
            g.memset(pair_ones[0:DH, 0:DH], 1.0)
            step.link(g.memset(pair_ones[DH:128, DH:128], 1.0))
            g.affine_select(out=ident[:, :], in_=ident[:, :], compare_op=ALU.not_equal, fill=1.0,
                            base=0, pattern=[[-1, 128]], channel_multiplier=1).then_inc(S["const_ready"], 1)
            pool.wait_ge(S["om_zeroed"], 1)
            for b in range(2):
                for t_, s_ in ((om_qb, om_q), (om_kb, om_k)):
                    pool.dma_start(t_[b * DH:(b + 1) * DH, b * DH:(b + 1) * DH], s_).then_inc(S["omega_loaded"], 16)
            PS = step.n + 1
            pool.wait_ge(S["stats_ready"], 1)
            step.link(g.tensor_scalar(rstd[:, :], ag[:, :, 1], LN_EPS, None, ALU.add))
            g.tensor_tensor(rstd[:, :], rstd[:, :], mhalf[:, :], ALU.pow).then_inc(S["rstd_ready"], 1)

            def rstd2(t):
                hold(pool, S["var2_ready"], t + 1, S["passed"])
                g.tensor_scalar(rstd[:, 0:1], ag[:, 0, 1:2], LN_EPS, None, ALU.add).then_inc(S["pool_step"], 1)
                pool.wait_ge(S["pool_step"], PS + 1 + t)
                g.tensor_tensor(rstd[:, 0:1], rstd[:, 0:1], mhalf[:, 0:1], ALU.pow).then_inc(S["rstd2_ready"], 1)

            def gelu_in(t):
                hold(pool, S["hd_stored"], t + 2, S["passed"])
                g.tensor_scalar(hu, hu, GELU_A, 1.0, ALU.mult, ALU.add).then_inc(S["gelu_step"], 1)
                pool.wait_ge(S["gelu_step"], 2 * t + 1)
                g.tensor_tensor(hu, hu, hx, ALU.mult).then_inc(S["gelu_u"], 1)

            def gelu_out(t):
                hold(pool, S["tanh_done"], t + 1, S["passed"])
                g.tensor_scalar(hu, hu, 0.5, 0.5, ALU.mult, ALU.add).then_inc(S["gelu_step"], 1)
                pool.wait_ge(S["gelu_step"], 2 * t + 2)
                g.tensor_tensor(gl[:, bass.ds(t % 2, 1), :].rearrange("p a n -> p (a n)"), hu, hx, ALU.mult)\
                    .then_inc(S["gelu_ready"], 1)

            def all_scores(t, half):
                hs = slice(half * FH // 2, (half + 1) * FH // 2)
                shp = [P, FH // 2, TOP, TOP]
                pool.wait_ge(S["ex1_done"], t + 1)
                pool.wait_ge(S["topv_ready"], 2 * t + half + 1)
                g.tensor_tensor(allsc[:, hs].rearrange("p h (a b) -> p h a b", a=TOP),
                                topv[:, hs].unsqueeze(3).to_broadcast(shp),
                                topf[:, hs].unsqueeze(2).to_broadcast(shp), ALU.add)\
                    .then_inc(S["all_ready"], 1)

            def diff(t):
                pool.wait_ge(S["ex2_done"], t + 2)
                g.tensor_tensor(ex1, ex1, ex2, ALU.subtract).then_inc(S["diff_ready"], 1)

            def gelu(t):
                gelu_in(t)
                gelu_out(t)

            rstd2(0)
            gelu(0)
            rstd2(1)
            all_scores(0, 0)
            all_scores(0, 1)
            with pool.Fori(1, T - 1) as t:
                gelu(t)
                diff(t - 1)
                rstd2(t + 1)
                all_scores(t, 0)
                all_scores(t, 1)
            gelu(T - 1)
            diff(T - 2)
            all_scores(T - 1, 0)
            all_scores(T - 1, 1)
            diff(T - 1)

        @block.scalar
        def _(act):
            a = nc.scalar
            for half in range(2):
                act.dma_start(keys_nat[:, half], keys[:, half * 128:(half + 1) * 128, 0, :].rearrange("h p d -> p h d"))\
                    .then_inc(S["keys_loaded"], 16)
            act.dma_start(wd_nat, w_down[0:NE, :].rearrange("(g p) d -> p g d", g=EC)).then_inc(S["wd_loaded"], 16)
            act.dma_start(wu_sb[:, :, :], w_up[0:NE, :].rearrange("(g p) d -> p g d", g=EC)).then_inc(S["wu_loaded"], 16)
            act.dma_start(bias_bc[:, :], bias.rearrange("(a d) -> a d", a=1).to_broadcast([P, D])).then_inc(S["bias_loaded"], 16)
            act.wait_ge(S["edges_transposed"], 1)
            for s in range(2):
                a.activation(edge_cols[:, s, :].rearrange("q (p a) -> q a p", p=NCH),
                             bank(s)[0:P, 0:CT * NCH].rearrange("q (a p) -> q a p", a=CT),
                             ACT.Copy).then_inc(S["edge_cols_ready"], 1)
            act.wait_ge(S["setup_transposed"], 1)
            a.activation(keysT[:, :, :], bank(2)[:, 0:2 * NK].rearrange("p (c k) -> p c k", c=2), ACT.Copy)
            a.activation(wdT[:, :, :], bank(3, 2).rearrange("p (c k) -> p c k", c=KC), ACT.Copy)\
                .then_inc(S["setup_stored"], 1)
            def transposed_out(t):
                act.wait_ge(S["xnT_psum"], t + 2)
                act.wait_ge(S["wc_psum"], t + 1)
                a.activation(x_stage[:, :, :], bank(3)[:, 0:KC * P].rearrange("p (k n) -> p k n", k=KC),
                             ACT.Copy).then_inc(S["x_staged"], 1)
                a.activation(xnT3[:, :, bass.ds(t * P, P)], bank(3)[:, 0:KC * P].rearrange("p (k n) -> p k n", k=KC),
                             ACT.Copy).then_inc(S["xnT_stored"], 1)

            def tile_out(t):
                act.wait_ge(S["adj_done"], t + 1)
                a.activation(adj[:, bass.ds(t, 1), :], psum[0:P, 0:N], ACT.Copy).then_inc(S["adj_stored"], 1)
                act.wait_ge(S["v_psum"], t + 1)
                a.activation(vaug[:, bass.ds(t, 1), :, 0:2 * DH].rearrange("p a c v -> p (a c) v"),
                             bank(4)[0:P].rearrange("p (c v) -> p c v", c=NPAIR), ACT.Copy).then_inc(S["v_stored"], 1)
                act.wait_ge(S["beta_psum"], t + 1)
                a.activation(beta[0:P, bass.ds(t, 1), :].rearrange("p a d -> p (a d)"), bank(5)[0:P],
                             ACT.Copy).then_inc(S["beta_stored"], 1)

            transposed_out(0)
            with act.Fori(0, T - 1) as t:
                tile_out(t)
                transposed_out(t + 1)
            tile_out(T - 1)

            def qk_out(c):
                act.wait_ge(S["q_psum"], c + 1)
                a.activation(qT, psum[:, 0:N], ACT.Copy, scale=Q_SCALE)
                a.activation(sqq, psum[:, 0:N], ACT.Square, scale=Q_SCALE).then_inc(S["q_stored"], 1)
                act.wait_ge(S["k_psum"], c + 1)
                a.activation(kT, bank(3, 3)[:, 0:N], ACT.Copy, scale=Q_SCALE)
                a.activation(sqk, bank(3, 3)[:, 0:N], ACT.Square, scale=Q_SCALE).then_inc(S["k_stored"], 1)

            def features_out(c):
                act.wait_ge(S["fk_min"], c + 1)
                a.activation(kphi, kphi, ACT.Exp).then_inc(S["fk_exp"], 1)
                act.wait_ge(S["ssk_max"], c + 1)
                a.activation(nk[:, :, :], nk[:, :, :], ACT.Exp, scale=-0.5).then_inc(S["ssk_exp"], 1)
                act.wait_ge(S["fq_min"], c + 1)
                a.activation(qphi, qphi, ACT.Exp).then_inc(S["fq_exp"], 1)
                act.wait_ge(S["ssq_max"], c + 1)
                a.activation(sqq, sqq, ACT.Exp, scale=-0.5).then_inc(S["ssq_exp"], 1)
                act.wait_ge(S["den_psum"], c + 1)
                a.activation(den_all, bank(3, 3)[:, 0:N], ACT.Copy)
                a.activation(num, psum[:, 0:N], ACT.Copy).then_inc(S["num_stored"], 1)

            qk_out(0)
            with act.Fori(0, NPAIR - 1) as c:
                features_out(c)
                qk_out(c + 1)
            features_out(NPAIR - 1)

            def front_stage(t):
                act.wait_ge(S["gnn_psum"], t + 1)
                a.activation(at_stage, adj[:, :, bass.ds(t * P, P)], ACT.Copy).then_inc(S["at_staged"], 1)

            def gelu(t):
                act.wait_ge(S["hd_psum"], t + 1)
                if not isinstance(t, int) or t > 0:
                    act.wait_ge(S["gelu_ready"], t)
                a.activation(hx, bank(1)[:, 0:EC * P], ACT.Copy)
                a.activation(hu, bank(1)[:, 0:EC * P], ACT.Square).then_inc(S["hd_stored"], 1)
                act.wait_ge(S["gelu_u"], t + 1)
                a.activation(hu, hu, ACT.Tanh, scale=GELU_C).then_inc(S["tanh_done"], 1)

            def weigh(t):
                act.wait_ge(S["den_ready"], t + 1)
                act.wait_ge(S["diff_ready"], t + 1)
                for h in range(FH):
                    last = a.activation(ex1[:, h], ex1[:, h], ACT.Copy, scale=rden[:, h:h + 1])
                last.then_inc(S["w_ready"], 1)

            def front(t):
                act.wait_ge(S["xn2T_psum"], t + 2)
                a.activation(xn2T, bank(2)[:, 0:KC * P].rearrange("p (k n) -> p k n", k=KC), ACT.Copy)\
                    .then_inc(S["xn2T_stored"], 1)
                act.wait_ge(S["q2_psum"], t + 1)
                a.activation(q2T, bank(3)[:, 0:KC * P].rearrange("p (k n) -> p k n", k=KC), ACT.Copy,
                             scale=BN_SCALE).then_inc(S["q2_stored"], 1)
                act.wait_ge(S["sim_psum"], t + 1)
                if not isinstance(t, int) or t > 0:
                    act.wait_ge(S["topv_ready"], 2 * t)
                a.activation(sim.rearrange("p (c b) e -> p b c e", c=2),
                             bank(4, 4)[0:P].rearrange("p (b c e) -> p b c e", b=4, c=2), ACT.Copy)\
                    .then_inc(S["sim_stored"], 1)

            def exps(t):
                act.wait_ge(S["negm_ready"], t + 1)
                act.wait_ge(S["st_psum"], t + 1)
                for h in range(FH):
                    last = a.activation(ex1[:, h], allsc[:, h], ACT.Exp, bias=negm[:, h:h + 1])
                last.then_inc(S["ex1_done"], 1)
                act.wait_ge(S["topd_ready"], t + 1)
                a.activation(topd, topd, ACT.Exp).then_inc(S["topd_exp"], 1)
                act.wait_ge(S["rest_ready"], t + 1)
                for h in range(FH):
                    last = a.activation(ex2[:, h], rest[:, h], ACT.Exp, bias=negm[:, h:h + 1])
                last.then_inc(S["ex2_done"], 1)

            for n, credit in (("hd_stored", 1), ("q2_stored", 1), ("sim_stored", 1), ("ex1_done", 1), ("ex2_done", 1)):
                act.sem_inc(S[n], credit)
            front_stage(0)
            act.wait_ge(S["wo_psum"], NPAIR * T)
            front(0)
            front_stage(1)
            gelu(0)
            front(1)
            exps(0)
            with act.Fori(1, T - 1) as t:
                front_stage(t + 1)
                gelu(t)
                weigh(t - 1)
                front(t + 1)
                exps(t)
            gelu(T - 1)
            weigh(T - 2)
            exps(T - 1)
            weigh(T - 1)

        @block.vector
        def _(dve):
            v = nc.vector
            step = Steps(dve, S["vec_step"])
            dve.wait_ge(S["edges_loaded"], 32)
            v.tensor_copy(edges_f, edges_i).then_inc(S["edges_float"], 1)
            dve.wait_ge(S["edges_float"], 1)
            v.tensor_reduce(ch_lim[:, 0:1], edges_f[:, 1, :], axis=AX.X, op=ALU.min)
            step.link(v.tensor_reduce(ch_lim[:, 1:2], edges_f[:, 1, :], axis=AX.X, op=ALU.max))
            dve.wait_ge(S["const_ready"], 1)
            shp = [NCH, T]
            v.tensor_tensor(touch[:, 0], blk_hi[:, :], ch_lim[:, 0:1].to_broadcast(shp), ALU.is_gt)
            step.link(v.tensor_tensor(touch[:, 1], blk_lo[:, :], ch_lim[:, 1:2].to_broadcast(shp), ALU.is_le))
            step.link(v.tensor_tensor(touch[:, 2], touch[:, 0], touch[:, 1], ALU.mult))
            v.tensor_tensor(cand[:, 0], touch[:, 2], ch_rank[:, 0:1].to_broadcast(shp), ALU.mult)
            v.tensor_tensor(cand[:, 1], touch[:, 2], ch_rank[:, 1:2].to_broadcast(shp), ALU.mult)\
                .then_inc(S["cand_ready"], 1)
            dve.wait_ge(S["x_loaded"], 16)
            for t in range(T):
                last = v.bn_stats(st[:, t, :], acc[:, t, :])
            step.link(last)
            for t in range(T):
                last = v.bn_aggr(ag[:, t, :], st[:, t, :])
            last.then_inc(S["stats_ready"], 1)
            dve.wait_ge(S["candT_ready"], 1)
            v.reduce_max(cand_max[:, :], bank(5)[0:2 * T, 0:NCH], AX.X).then_inc(S["cand_max_ready"], 1)
            dve.wait_ge(S["cand_row_ready"], 1)
            step.link(v.tensor_copy(rng[0:1, 0:2, :], bank(6)[0:1, 0:2 * T].rearrange("p (k j) -> p k j", k=2)))
            step.link(v.tensor_scalar(rng[0:1, 2, :], rng[0:1, 1, :], -1.0, float(NCH), ALU.mult, ALU.add))
            step.link(v.tensor_scalar(rng[0:1, 2, :], rng[0:1, 2, :], float(NCH - 1), None, ALU.min))
            step.link(v.tensor_scalar(rng[0:1, 3, :], rng[0:1, 2, :], 1.0, None, ALU.add))
            step.link(v.tensor_tensor(rng[0:1, 3, :], rng[0:1, 3, :], rng[0:1, 0, :], ALU.max))
            step.link(v.tensor_tensor(rng[0:1, 4, :], rng[0:1, 3, :], rng[0:1, 2, :], ALU.subtract))
            step.link(v.tensor_tensor_scan(rng[0:1, 5, :], rng[0:1, 4, :], rng[0:1, 4, :], 0.0, ALU.add, ALU.max))
            step.link(v.tensor_tensor(rng[0:1, 6, :], rng[0:1, 5, :], rng[0:1, 4, :], ALU.subtract))
            v.tensor_copy(rng_i[0:1, 0, :], rng[0:1, 6, :])
            v.tensor_copy(rng_i[0:1, 1, :], rng[0:1, 5, :])
            v.tensor_copy(rng_i[0:1, 2, :], rng[0:1, 2, :]).then_inc(S["ranges_ready"], 1)

            dve.wait_ge(S["rstd_ready"], 1)
            dve.wait_ge(S["bias_loaded"], 16)
            dve.wait_ge(S["ranges_ready"], 1)
            dve.wait_ge(S["edge_cols_ready"], 2)
            for k in range(CT):
                dve.sem_inc(hot_ready[k], 1)
            dve.sem_inc(S["wc_added"], 1)
            def normalised(j):
                at = tile_of(j)
                dve.wait_ge(S["xnT_psum"], j + 1)
                v.tensor_scalar(xn_tile, at, ag[:, bass.ds(j, 1), 0], rstd[:, bass.ds(j, 1)],
                                ALU.subtract, ALU.mult).then_inc(S["xn_ready"], 1)
                dve.wait_ge(S["xn_ready"], j + 1)
                v.tensor_tensor(at, at, bias_bc[:, :], ALU.add).then_inc(S["mix_step"], 1)

            def one_hots(j):
                lo = load_range(dve, 0, j)
                hi = load_range(dve, 1, j)
                ch0 = load_range(dve, 2, j)
                with dve.Fori(lo, hi) as slot:
                    e0 = nc.s_assert_within((slot - lo + ch0) * CT, 0, (NCH - 1) * CT,
                                            skip_runtime_bounds_check_because="the ranges are clamped to the chunks")
                    side = dve.snap((slot % 2) * CT)
                    turn = dve.snap(slot + 1)
                    for k in range(CT):
                        dve.wait_ge(hot_free[k], turn)
                        v.tensor_scalar(hot_dst[:, bass.ds(side + k, 1), :], iota[:, bass.ds(j * P, P)],
                                        edge_cols[:, 1, bass.ds(e0 + k, 1)], None, ALU.is_equal)
                        v.tensor_scalar(hot_src[:, bass.ds(side + k, 1), :], iota[:, :], edge_cols[:, 0, bass.ds(e0 + k, 1)], None,
                                        ALU.is_equal).then_inc(hot_ready[k], 1)

            def add_wc(j):
                dve.wait_ge(S["mix_step"], j + 1)
                dve.wait_ge(S["wc_psum"], j + 2)
                v.tensor_tensor(tile_of(j), tile_of(j), bank67(j), ALU.add).then_inc(S["wc_added"], 1)

            normalised(0)
            one_hots(0)
            normalised(1)
            with dve.Fori(1, T - 1) as j:
                one_hots(j)
                add_wc(j - 1)
                normalised(j + 1)
            one_hots(T - 1)
            add_wc(T - 2)
            add_wc(T - 1)
            dve.wait_ge(S["adj_stored"], T + 1)
            v.reduce_sum(col_sum[:, :], adj[:, :, :].rearrange("p t n -> p n t"), AX.X).then_inc(S["col_summed"], 1)

            MS = 1

            def add_wo(c, ts):
                for t in ts:
                    dve.wait_ge(S["wo_psum"], c * T + t + 1)
                    if t == 0:
                        dve.wait_ge(S["wo_added"], c * T + 1)
                    v.tensor_tensor(acc[:, t, :], acc[:, t, :], bank(6 + t % 2)[0:P], ALU.add)\
                        .then_inc(S["wo_added"], 1)

            def features(c, first=False):
                m = Steps(dve, S["mix_step"], T + MS * c)
                dve.wait_ge(S["fq_psum"], c + 1)
                v.tensor_scalar(qphi, psum[:, 0:N], CLAMP, None, ALU.min).then_inc(S["fq_min"], 1)
                dve.wait_ge(S["fk_psum"], c + 1)
                v.tensor_scalar(kphi, bank(3, 3)[0:P, 0:T * 128].rearrange("p (t m) -> p t m", t=T), CLAMP, None,
                                ALU.min).then_inc(S["fk_min"], 1)
                dve.wait_ge(S["ssk_psum"], c + 1)
                v.tensor_scalar(nk[:, :, :], bank(6)[0:P, 0:2 * T].rearrange("p (t h) -> p t h", h=2), EPS * EPS,
                                None, ALU.max).then_inc(S["ssk_max"], 1)
                dve.wait_ge(S["ssq_psum"], c + 1)
                v.tensor_scalar(sqq, psum[:, 0:N], EPS * EPS, None, ALU.max).then_inc(S["ssq_max"], 1)
                if not first:
                    add_wo(c - 1, range(0, 3))
                dve.wait_ge(S["ssk_exp"], c + 1)
                m.link(v.tensor_scalar(nk[:, :, :], nk[:, :, :], EPS, None, ALU.max))
                dve.wait_ge(S["fk_exp"], c + 1)
                v.tensor_tensor(kphi.rearrange("p t (h m) -> p t h m", h=2),
                                kphi.rearrange("p t (h m) -> p t h m", h=2),
                                nk[:, :, :].unsqueeze(3).to_broadcast([P, T, 2, DH]), ALU.mult)\
                    .then_inc(S["kphi_ready"], 1)
                if not first:
                    add_wo(c - 1, range(3, 5))
                dve.wait_ge(S["ssq_exp"], c + 1)
                dve.wait_ge(S["fq_exp"], c + 1)
                v.scalar_tensor_tensor(qphi, sqq, EPS, qphi, ALU.max, ALU.mult).then_inc(S["qphi_ready"], 1)
                if not first:
                    add_wo(c - 1, range(5, T))
                dve.wait_ge(S["kv_psum"], c + 1)
                kv = bank(7)
                v.tensor_copy(kv_blk[0:DH, 0:DH], kv[0:DH, 0:DH])
                v.tensor_copy(kv_blk[DH:128, DH:128], kv[DH:128, DH:2 * DH])
                v.tensor_copy(ones_blk[0:DH, 0:DH], kv[0:DH, VC - 1:VC].to_broadcast([DH, DH]))
                v.tensor_copy(ones_blk[DH:128, DH:128], kv[DH:128, VC - 1:VC].to_broadcast([DH, DH]))\
                    .then_inc(S["kv_stored"], 1)
                dve.wait_ge(S["num_stored"], c + 1)
                v.reciprocal(den_all, den_all).then_inc(S["den_inv"], 1)
                dve.wait_ge(S["den_inv"], c + 1)
                v.tensor_tensor(num, num, den_all, ALU.mult).then_inc(S["attn_ready"], 1)
                assert m.n == MS

            features(0, first=True)
            with dve.Fori(1, NPAIR) as c:
                features(c)
            add_wo(NPAIR - 1, range(T))
            dve.wait_ge(S["count_psum"], 1)
            v.reciprocal(rcnt[:, :], bank(2)[0:P, 512 - T:512]).then_inc(S["count_inv"], 1)
            dve.wait_ge(S["count_inv"], 1)

            XS = 2

            class Residual:

                def __init__(self, t):
                    self.t, self.at, self.base = t, tile_of(t), XS * t

                def add(self):
                    dve.wait_ge(S["gnn_psum"], self.t + 2)
                    v.scalar_tensor_tensor(self.at, bank(1)[0:P], rcnt[:, bass.ds(self.t, 1)], self.at, ALU.mult, ALU.add)\
                        .then_inc(S["x1_step"], 1)

                def stats(self):
                    hold(dve, S["x1_step"], self.base + 1, S["passed"])
                    v.bn_stats(st[:, 0, :], self.at).then_inc(S["x1_step"], 1)

                def aggregate(self):
                    hold(dve, S["x1_step"], self.base + 2, S["passed"])
                    v.bn_aggr(ag[:, 0, :], st[:, 0, :]).then_inc(S["var2_ready"], 1)

                def normalise(self):
                    dve.wait_ge(S["xn2T_psum"], self.t + 1)
                    dve.wait_ge(S["rstd2_ready"], self.t + 1)
                    v.tensor_scalar(xn_tile, self.at, ag[:, 0, 0:1], rstd[:, 0:1], ALU.subtract, ALU.mult)\
                        .then_inc(S["xn2_ready"], 1)

            halves = [range(0, FH // 2), range(FH // 2, FH)]
            KS = 10

            def top_keys(t, between):
                stages = [lambda h: v.max(topv[:, h, 0:8], sim[:, h]),
                          lambda h: v.max_index(topi[:, h, 0:8], topv[:, h, 0:8], sim[:, h]),
                          lambda h: v.match_replace(sim[:, h], topv[:, h, 0:8], sim[:, h], LOWEST),
                          lambda h: v.max(topv[:, h, 8:16], sim[:, h]),
                          lambda h: v.max_index(topi[:, h, 8:16], topv[:, h, 8:16], sim[:, h])]
                hold(dve, S["sim_stored"], t + 2, S["passed"])
                if not isinstance(t, int) or t > 0:
                    hold(dve, S["all_ready"], 2 * t, S["passed"])
                for n, stage in enumerate(stages):
                    for half in range(2):
                        if n:
                            hold(dve, S["topk_step"], KS * t + 2 * n - 1 + half, S["passed"])
                        for h in halves[half]:
                            last = stage(h)
                        last.then_inc(S["topk_step"], 1)
                        for step_ in between.get((n, half), []):
                            step_()
                for half in range(2):
                    dve.wait_ge(S["topk_step"], KS * t + KS - 1 + half)
                    hs = slice(half * FH // 2, (half + 1) * FH // 2)
                    v.tensor_copy(topf[:, hs], topi[:, hs]).then_inc(S["topv_ready"], 1)

            SS = 6

            def top_scores(t):
                for half in range(2):
                    hold(dve, S["all_ready"], 2 * t + half + 1, S["passed"])
                    for h in halves[half]:
                        last = v.max(tops[:, h, 0:8], allsc[:, h])
                    last.then_inc(S["score_step"], 1)
                hold(dve, S["ex2_done"], t + 1, S["passed"])
                for half in range(2):
                    hold(dve, S["score_step"], SS * t + 1 + half, S["passed"])
                    if half:
                        v.tensor_scalar(negm, tops[:, :, 0], -1.0, None, ALU.mult).then_inc(S["negm_ready"], 1)
                    for h in halves[half]:
                        last = v.match_replace(rest[:, h], tops[:, h, 0:8], allsc[:, h], LOWEST)
                    last.then_inc(S["score_step"], 1)
                for half in range(2):
                    hold(dve, S["score_step"], SS * t + 3 + half, S["passed"])
                    for h in halves[half]:
                        last = v.max(tops[:, h, 8:16], rest[:, h])
                    last.then_inc(S["score_step"], 1)
                for half in range(2):
                    hold(dve, S["score_step"], SS * t + 5 + half, S["passed"])
                    if half:
                        v.tensor_tensor(topd, tops, negm.unsqueeze(2).to_broadcast([P, FH, TOP]), ALU.add)\
                            .then_inc(S["topd_ready"], 1)
                    for h in halves[half]:
                        last = v.match_replace(rest[:, h], tops[:, h, 8:16], rest[:, h], LOWEST)
                last.then_inc(S["rest_ready"], 1)

            def den_sum(t):
                dve.wait_ge(S["topd_exp"], t + 1)
                v.reduce_sum(den, topd, AX.X).then_inc(S["sel_step"], 1)

            def den_invert(t):
                dve.wait_ge(S["sel_step"], t + 1)
                v.reciprocal(rden, den).then_inc(S["den_ready"], 1)

            def combine(t):
                dve.wait_ge(S["st_psum"], t + 2)
                dve.wait_ge(S["gelu_ready"], t + 1)
                v.tensor_tensor(comT.rearrange("p k n -> p (k n)"), bank(0)[:, 0:EC * P],
                                gl[:, bass.ds(t % 2, 1), :].rearrange("p a n -> p (a n)"), ALU.mult)\
                    .then_inc(S["com_ready"], 1)

            def add_out(t):
                dve.wait_ge(S["out_psum"], t + 1)
                v.tensor_tensor(tile_of(t), tile_of(t), bank(3)[0:P], ALU.add).then_inc(S["out_ready"], 1)

            dve.sem_inc(S["out_ready"], 1)
            r = Residual(0)
            for step_ in (r.add, r.stats, r.aggregate, r.normalise):
                step_()

            def tile(t, res=True, den_of=None, out_of=None):
                between = {}

                def put(n, half, f):
                    between.setdefault((n, half), []).append(f)

                if den_of is not None:
                    put(0, 0, lambda: den_sum(den_of))
                    put(0, 1, lambda: den_invert(den_of))
                if out_of is not None:
                    put(2, 1, lambda: add_out(out_of))
                if res:
                    r = Residual(t + 1)
                    put(3, 1, r.add)
                    put(4, 0, r.stats)
                    put(4, 1, r.aggregate)
                top_keys(t, between)
                if res:
                    r.normalise()
                if den_of is not None:
                    combine(den_of)
                top_scores(t)

            tile(0)
            tile(1, den_of=0)
            with dve.Fori(2, T - 1) as t:
                tile(t, den_of=t - 1, out_of=t - 2)
            tile(T - 1, res=False, den_of=T - 2, out_of=T - 3)
            add_out(T - 2)
            den_sum(T - 1)
            den_invert(T - 1)
            combine(T - 1)
            add_out(T - 1)

        @block.tensor
        def _(pe):
            te = nc.tensor
            pe.wait_ge(S["const_ready"], 1)
            pe.wait_ge(S["edges_float"], 1)
            for s in range(2):
                for k in range(CT):
                    last = te.transpose(bank(s)[0:P, k * NCH:(k + 1) * NCH], edges_f[:, s, k * P:(k + 1) * P],
                                        ident[0:NCH, 0:NCH])
            last.then_inc(S["edges_transposed"], 1)
            pe.wait_ge(S["cand_ready"], 1)
            te.transpose(bank(5)[0:2 * T, 0:NCH], cand[:, :, :].rearrange("p k j -> p (k j)"),
                         ident[0:NCH, 0:NCH]).then_inc(S["candT_ready"], 1)
            pe.wait_ge(S["cand_max_ready"], 1)
            te.transpose(bank(6)[0:1, 0:2 * T], cand_max[:, :], ident[0:2 * T, 0:2 * T])\
                .then_inc(S["cand_row_ready"], 1)
            pe.wait_ge(S["keys_loaded"], 32)
            for c in range(2):
                for gk in range(2):
                    te.transpose(bank(2)[:, c * NK + gk * 128:c * NK + (gk + 1) * 128],
                                 keys_nat[:, gk, 4 * c:4 * c + 4, :].rearrange("p h d -> p (h d)"), ident[:, :])
            pe.wait_ge(S["wd_loaded"], 16)
            for c in range(KC):
                for gk in range(EC):
                    last = te.transpose(bank(3, 2)[:, c * NE + gk * 128:c * NE + (gk + 1) * 128],
                                        wd_nat[:, gk, c * 128:(c + 1) * 128], ident[:, :])
            last.then_inc(S["setup_transposed"], 1)
            pe.wait_ge(S["setup_stored"], 1)
            pe.wait_ge(S["edge_cols_ready"], 2)
            pe.wait_ge(S["ranges_ready"], 1)
            pe.wait_ge(S["wv_loaded"], 16)
            pe.wait_ge(S["wn_loaded"], 16)
            pe.wait_ge(S["wc_loaded"], 16)
            for s in ("xnT_psum", "wc_psum", "v_stored", "beta_stored", "xnT_stored", "adj_stored", "wc_added"):
                pe.sem_inc(S[s], 1)
            for k in range(CT):
                pe.sem_inc(hot_free[k], 2)

            def transposed(j):
                pe.wait_ge(S["xn_ready"], j + 1)
                pe.wait_ge(S["xnT_stored"], j + 1)
                for k in range(KC):
                    last = te.transpose(bank(3)[:, k * P:(k + 1) * P], xn_tile[:, k * 128:(k + 1) * 128],
                                        ident[0:P, 0:P])
                last.then_inc(S["xnT_psum"], 1)

            def adjacency(j):
                lo = load_range(pe, 0, j)
                hi = load_range(pe, 1, j)
                pe.wait_ge(S["adj_stored"], j + 1)
                for lo_, hi_ in banks:
                    te.matmul(psum[0:P, lo_:hi_], zrow[0:1, 0:P], zrow[0:1, 0:hi_ - lo_], start=True, stop=False)
                with pe.Fori(lo, hi) as slot:
                    side = pe.snap((slot % 2) * CT)
                    for k in range(CT):
                        pe.wait_ge(hot_ready[k], slot + 2)
                        for lo_, hi_ in banks:
                            last = te.matmul(psum[0:P, lo_:hi_],
                                             hot_dst[:, bass.ds(side + k, 1), :].rearrange("p a n -> p (a n)"),
                                             hot_src[:, bass.ds(side + k, 1), lo_:hi_].rearrange("p a n -> p (a n)"),
                                             start=False, stop=False)
                        last.then_inc(hot_free[k], 1)
                for lo_, hi_ in banks:
                    last = te.matmul(psum[0:P, lo_:hi_], zrow[0:1, 0:P], zrow[0:1, 0:hi_ - lo_], start=False, stop=True)
                last.then_inc(S["adj_done"], 1)

            def token_products(j):
                pe.wait_ge(S["x_staged"], j + 1)
                for to, w, s, free in ((bank(4)[0:P], Wv_sb, "v_psum", "v_stored"),
                                       (bank(5)[0:P], wn_sb, "beta_psum", "beta_stored"),
                                       (bank67(j), wc_sb, "wc_psum", "wc_added")):
                    pe.wait_ge(S[free], j + 1)
                    for k in range(KC):
                        last = te.matmul(to, x_stage[:, k, :], w[:, k, :], start=(k == 0), stop=(k == KC - 1))
                    last.then_inc(S[s], 1)

            transposed(0)
            with pe.Fori(0, T - 1) as j:
                adjacency(j)
                token_products(j)
                transposed(j + 1)
            adjacency(T - 1)
            token_products(T - 1)

            pe.wait_ge(S["xnT_stored"], T + 1)
            pe.wait_ge(S["v_stored"], T + 1)
            pe.wait_ge(S["beta_stored"], T + 1)
            pe.wait_ge(S["wc_added"], T + 2)
            pe.wait_ge(S["adj_stored"], T + 1)
            pe.wait_ge(S["omega_loaded"], 64)
            pe.wait_ge(S["wo_loaded"], 16)
            pe.sem_inc(S["wo_added"], 1)

            def project(c):
                pe.wait_ge(S["pair_loaded"], c * 32 + 32)
                if not isinstance(c, int) or c > 0:
                    pe.wait_ge(S["num_stored"], c)
                for i, s in enumerate(("q_psum", "k_psum")):
                    for lo_, hi_ in banks:
                        for k in range(KC):
                            last = te.matmul(bank(3 * i, 3)[:, lo_:hi_], w_pair[:, i, k, :], xnT3[:, k, lo_:hi_],
                                             start=(k == 0), stop=(k == KC - 1))
                    last.then_inc(S[s], 1)

            def feature_products(c):
                pe.wait_ge(S["q_stored"], c + 1)
                for lo_, hi_ in banks:
                    last = te.matmul(psum[:, lo_:hi_], om_qb[:, :], qT[:, lo_:hi_], start=True, stop=True)
                last.then_inc(S["fq_psum"], 1)
                pe.wait_ge(S["k_stored"], c + 1)
                for t in range(T):
                    last = te.matmul(bank(3, 3)[0:P, t * 128:(t + 1) * 128], kT[:, t * P:(t + 1) * P], om_kb[:, :],
                                     start=True, stop=True)
                last.then_inc(S["fk_psum"], 1)
                if not isinstance(c, int) or c > 1:
                    pe.wait_ge(S["wo_added"], (c - 1) * T + 1)
                for t in range(T):
                    last = te.matmul(bank(6)[0:P, 2 * t:2 * t + 2], sqk[:, t * P:(t + 1) * P],
                                     pair_ones[:, DH - 1:DH + 1], start=True, stop=True)
                last.then_inc(S["ssk_psum"], 1)
                pe.wait_ge(S["fq_min"], c + 1)
                for lo_, hi_ in banks:
                    last = te.matmul(psum[:, lo_:hi_], pair_ones[:, :], sqq[:, lo_:hi_], start=True, stop=True)
                last.then_inc(S["ssq_psum"], 1)

            def attention(c):
                pe.wait_ge(S["kphi_ready"], c + 1)
                if not isinstance(c, int) or c > 0:
                    pe.wait_ge(S["wo_added"], c * T + 1)
                for t in range(T):
                    last = te.matmul(bank(7)[:, 0:VC], kphi[:, t, :],
                                     vaug[:, t, bass.ds(c, 1), :].rearrange("p a v -> p (a v)"),
                                     start=(t == 0), stop=(t == T - 1))
                last.then_inc(S["kv_psum"], 1)
                pe.wait_ge(S["kv_stored"], c + 1)
                pe.wait_ge(S["qphi_ready"], c + 1)
                for lo_, hi_ in banks:
                    te.matmul(bank(3, 3)[:, lo_:hi_], ones_blk[:, :], qphi[:, lo_:hi_], start=True, stop=True)
                for lo_, hi_ in banks:
                    last = te.matmul(psum[:, lo_:hi_], kv_blk[:, :], qphi[:, lo_:hi_], start=True, stop=True)
                last.then_inc(S["den_psum"], 1)

            def output(c):
                if not isinstance(c, int) or c < NPAIR - 1:
                    pe.wait_ge(S["ssk_max"], c + 2)
                pe.wait_ge(S["attn_ready"], c + 1)
                for t in range(T):
                    if t >= 2:
                        pe.wait_ge(S["wo_added"], c * T + t)
                    te.matmul(bank(6 + t % 2)[0:P], num[:, t * P:(t + 1) * P],
                              Wo_sb[:, bass.ds(c, 1), :].rearrange("p a d -> p (a d)"),
                              start=True, stop=True).then_inc(S["wo_psum"], 1)

            project(0)
            feature_products(0)
            attention(0)
            project(1)
            with pe.Fori(1, NPAIR - 1) as c:
                feature_products(c)
                output(c - 1)
                attention(c)
                project(c + 1)
            feature_products(NPAIR - 1)
            output(NPAIR - 2)
            attention(NPAIR - 1)

            def gnn(t):
                pe.wait_ge(S["at_staged"], t + 1)
                pe.wait_ge(S["hd_stored"], t + 1)
                for j in range(T):
                    last = te.matmul(bank(1)[0:P], at_stage[:, j, :], beta[0:P, j, :], start=(j == 0), stop=(j == T - 1))
                last.then_inc(S["gnn_psum"], 1)

            def front(t):
                pe.wait_ge(S["xn2_ready"], t + 1)
                for k in range(KC):
                    last = te.transpose(bank(2)[:, k * P:(k + 1) * P], xn_tile[:, k * 128:(k + 1) * 128],
                                        ident[0:P, 0:P])
                last.then_inc(S["xn2T_psum"], 1)
                if not isinstance(t, int) or t > 1:
                    pe.wait_ge(S["out_ready"], t - 1)
                pe.wait_ge(S["xn2T_stored"], t + 1)
                for m in range(KC):
                    for k in range(KC):
                        last = te.matmul(bank(3)[:, m * P:(m + 1) * P], wf_sb[:, k, m * 128:(m + 1) * 128],
                                         xn2T[:, k, :], start=(k == 0), stop=(k == KC - 1))
                last.then_inc(S["q2_psum"], 1)
                pe.wait_ge(S["q2_stored"], t + 2)
                pe.wait_ge(S["sim_stored"], t + 1)
                for h in range(FH):
                    c, b = h // 4, h % 4
                    last = te.matmul(bank(4 + b)[0:P, c * NK:(c + 1) * NK], q2T[b * DK:(b + 1) * DK, c, :],
                                     keysT[b * DK:(b + 1) * DK, c, :], start=True, stop=True)
                last.then_inc(S["sim_psum"], 1)
                for g in range(EC):
                    for k in range(KC):
                        last = te.matmul(bank(1)[:, g * P:(g + 1) * P], wdT[:, k, g * 128:(g + 1) * 128],
                                         q2T[:, k, :], start=(k == 0), stop=(k == KC - 1))
                last.then_inc(S["hd_psum"], 1)

            def sum_heads(t):
                pe.wait_ge(S["w_ready"], t + 1)
                for g in range(EC):
                    for h in range(FH):
                        last = te.matmul(bank(0)[:, g * P:(g + 1) * P], ex1[:, h, g * 128:(g + 1) * 128],
                                         ident[0:P, 0:P], start=(h == 0), stop=(h == FH - 1))
                last.then_inc(S["st_psum"], 1)

            def outputs(t):
                pe.wait_ge(S["com_ready"], t + 1)
                for k in range(EC):
                    last = te.matmul(bank(3)[0:P], comT[:, k, :], wu_sb[:, k, :], start=(k == 0), stop=(k == EC - 1))
                last.then_inc(S["out_psum"], 1)

            pe.wait_ge(S["wf_loaded"], 16)
            pe.wait_ge(S["wu_loaded"], 16)
            pe.wait_ge(S["num_stored"], NPAIR)
            pe.sem_inc(S["gnn_psum"], 1)
            pe.sem_inc(S["xn2T_psum"], 1)
            pe.sem_inc(S["st_psum"], 1)
            pe.wait_ge(S["col_summed"], 1)
            for t in range(T):
                last = te.matmul(bank(2)[0:P, 512 - T + t:512 - T + t + 1], col_sum[:, t * P:(t + 1) * P], ones1[:, 0:1],
                                 start=True, stop=True)
            last.then_inc(S["count_psum"], 1)
            gnn(0)
            output(NPAIR - 1)
            pe.wait_ge(S["wo_added"], NPAIR * T + 1)
            front(0)
            gnn(1)
            front(1)
            with pe.Fori(1, T - 1) as t:
                gnn(t + 1)
                sum_heads(t - 1)
                front(t + 1)
                outputs(t - 1)
            sum_heads(T - 2)
            outputs(T - 2)
            sum_heads(T - 1)
            outputs(T - 1)


_INS = ["x", "src", "dst", "L0_gnn_wc", "L0_gnn_wn", "L0_gnn_bias", "L0_mix_Wq", "L0_mix_Wk", "L0_mix_Wv", "L0_mix_Wo",
        "L0_mix_omega_q", "L0_mix_omega_k", "L0_ffn_w_q", "L0_ffn_keys", "L0_ffn_weight_down_embed",
        "L0_ffn_weight_up_embed"]


def kernel(**inputs):
    import numpy as _np
    import concourse.bacc as _bacc
    from concourse import mybir as _mybir
    from concourse.bass_utils import run_bass_kernel_spmd as _run

    nc = _bacc.Bacc("TRN2", target_bir_lowering=False, num_devices=1)
    arrays, args = {}, []
    for name in _INS:
        a = _np.ascontiguousarray(inputs[name])
        arrays[f"in_{name}_dram"] = a
        args.append(nc.dram_tensor(f"in_{name}_dram", a.shape, _mybir.dt.from_np(a.dtype), kind="ExternalInput").ap())
    shape = inputs["x"].shape
    out = nc.dram_tensor("out_dram", shape, _mybir.dt.float32, kind="ExternalOutput").ap()
    gps_layer(nc, *args, out)
    r = _run(nc, [arrays], core_ids=[0])
    return r.results[0]["out_dram"]
```

```python
import concourse.bass as bass
from concourse import mybir
from contextlib import ExitStack, contextmanager

FP32 = mybir.dt.float32
FP16 = mybir.dt.float16
I32 = mybir.dt.int32
U32 = mybir.dt.uint32
U16 = mybir.dt.uint16
ALU = mybir.AluOpType
ACT = mybir.ActivationFunctionType
AX = mybir.AxisListType


def hold(eng, sem, value, passed):
    eng.wait_ge(sem, value)
    eng.sem_inc(passed, 1)


class Steps:

    def __init__(self, eng, sem, base=0, passed=None):
        self.eng, self.sem, self.base, self.n, self.passed = eng, sem, base, 0, passed

    def link(self, ins):
        self.n += 1
        ins.then_inc(self.sem, 1)
        if self.passed is None:
            self.eng.wait_ge(self.sem, self.base + self.n)
        else:
            hold(self.eng, self.sem, self.base + self.n, self.passed)




def gps_layer(nc, x, src, dst, wc, wn, bias, Wq, Wk, Wv, Wo, om_q, om_k, wf, keys, w_down, w_up, out):
    N, D = x.shape
    E = src.shape[0]
    P = 125
    T = N // P
    KC = D // 128
    H = 8
    DH = D // H
    NPAIR = H // 2
    VC = 2 * DH + 1
    CT = 4
    CH = CT // 2
    UNIT = 1.0 / 8
    RING = 4
    NCH = E // P // CT
    FH = keys.shape[0]
    NK = keys.shape[1]
    DK = keys.shape[3]
    TOP = 16
    NE = TOP * TOP
    EC = NE // 128
    Q_SCALE = 1.0 / DH ** 0.5
    BN_SCALE = 1.0 / (1.0 + 1e-5) ** 0.5
    LN_EPS = 1e-5
    EPS = 1e-8
    CLAMP = 50.0
    LOWEST = -3.0e38
    GELU_C = 0.7978845608028654
    GELU_A = 0.044715
    banks = [(0, 512), (512, 1024), (1024, N)]

    ctx = ExitStack()
    with ctx:
        def sb(name, shape, dt=FP32):
            return ctx.enter_context(nc.sbuf_tensor(name, shape, dt))

        def sem(name):
            return ctx.enter_context(nc.semaphore(name))

        ident = sb("ident", [128, 128])
        pair_ones = sb("pair_ones", [128, 128])
        iota = sb("iota", [P, N], FP16)
        zrow = sb("zrow", [1, 512], FP16)
        om_qb = sb("om_qb", [128, 128])
        om_kb = sb("om_kb", [128, 128])
        acc = sb("acc", [P, T, D])
        beta = sb("beta", [128, T, D])
        W = sb("W", [128, 4, KC, D])
        wf_sb = sb("wf_sb", [128, KC, D])
        wu_sb = sb("wu_sb", [128, EC, D])
        wdT = sb("wdT", [128, KC, NE])
        keysT = sb("keysT", [128, 2, NK])
        bias_bc = sb("bias_bc", [P, D])
        xnT = sb("xnT", [128, KC * N])
        adj = sb("adj", [P, T, N], U16)
        vaug = sb("vaug", [P, T, NPAIR, VC])
        work = sb("work", [128, 4 * N + T * 128])
        hot_dst = sb("hot_dst", [P, CT, P], FP16)
        col_sum = sb("col_sum", [P, N])
        w_pair = sb("w_pair", [128, 2, KC, 128])
        x_stage = sb("x_stage", [128, KC, P])
        kv_blk = sb("kv_blk", [128, 128])
        ones_blk = sb("ones_blk", [128, 128])
        edge_cols = sb("edge_cols", [P, 2, NCH * CT])
        ch_lim = sb("ch_lim", [NCH, 2])
        ch_rank = sb("ch_rank", [NCH, 2])
        blk_lo = sb("blk_lo", [NCH, T])
        blk_hi = sb("blk_hi", [NCH, T])
        touch = sb("touch", [NCH, 3, T])
        cand = sb("cand", [NCH, 2, T])
        cand_max = sb("cand_max", [2 * T, 1])
        rng = sb("rng", [1, 8, T])
        rng_i = sb("rng_i", [1, 3, T], I32)
        st = sb("st", [P, 6])
        ag = sb("ag", [P, 2])
        rstd = sb("rstd", [P, 1])
        mhalf = sb("mhalf", [P, 1])
        nk = sb("nk", [P, T, 2])
        rcnt = sb("rcnt", [P, T])
        ones1 = sb("ones1", [P, 2])

        xnT3 = xnT[:, 0:KC * N].rearrange("p (k n) -> p k n", k=KC)
        Wv_sb, wn_sb, wc_sb, Wo_sb = (W[:, i] for i in range(4))
        qT, kT, sqq = (work[:, i * N:(i + 1) * N] for i in range(3))
        W_used = W[:, 0:3].rearrange("p a k d -> p (a k d)")
        qphi, num, den_all = (W_used[:, i * N:(i + 1) * N] for i in range(3))
        sqk = work[:, 3 * N:4 * N]
        kphi = work[0:P, 4 * N:4 * N + T * 128].rearrange("p (t m) -> p t m", t=T)
        edges_i = work[0:NCH, N:N + 2 * CT * P].bitcast(I32).rearrange("p (s e) -> p s e", s=2)
        edges_f = work[0:NCH, N + 2 * CT * P:N + 4 * CT * P].rearrange("p (s e) -> p s e", s=2)
        at_stage = kT[0:P, :].rearrange("p (j s) -> p j s", j=T)
        dst_off = col_sum[:, 0:RING * CT * P // 2].bitcast(FP16).rearrange("p (k n) -> p k n", k=RING * CT)
        hot_src = work[0:P, N:N + CT * N // 2].bitcast(FP16).rearrange("p (k n) -> p k n", k=CT)
        xn_tile = qT[0:P, 0:D]
        sum_tile, out_tile = (sqq[0:P, i * D:(i + 1) * D] for i in range(2))
        wd_nat = beta[:, 0:EC, :]
        keys_nat = beta[:, EC, :].rearrange("p (g h d) -> p g h d", g=2, h=FH)
        ffn = W[:, 0:4].rearrange("p a k d -> p (a k d)")
        sim, allsc, rest, ex1 = (ffn[0:P, i * FH * NK:(i + 1) * FH * NK].rearrange("p (h e) -> p h e", h=FH)
                                 for i in range(4))
        ex2 = xnT[0:P, 0:FH * NK].rearrange("p (h e) -> p h e", h=FH)
        o = FH * NK

        def cut(n, rows=128):
            nonlocal o
            o += n
            return xnT[0:rows, o - n:o]

        xn2T = cut(KC * P).rearrange("p (k n) -> p k n", k=KC)
        q2T = cut(KC * P).rearrange("p (k n) -> p k n", k=KC)
        comT = cut(EC * P).rearrange("p (k n) -> p k n", k=EC)
        hx, hu = (cut(EC * P) for _ in range(2))
        gl = cut(2 * EC * P).rearrange("p (g n) -> p g n", g=2)
        o2 = 0

        def cut2(n):
            nonlocal o2
            o2 += n
            return work[0:P, 3 * N + o2 - n:3 * N + o2]

        topv, topf, tops, topd = (cut2(FH * TOP).rearrange("p (h k) -> p h k", h=FH) for _ in range(4))
        topi = cut2(FH * TOP).bitcast(U32).rearrange("p (h k) -> p h k", h=FH)
        negm, den, rden = (cut2(FH) for _ in range(3))

        psum = ctx.enter_context(nc.psum_tensor("psum", [128, 8 * 512], FP32))

        def bank(b, n=1):
            return psum[:, b * 512:(b + n) * 512]

        heads = [range(0, FH // 2), range(FH // 2, FH)]
        halves = [slice(0, FH // 2), slice(FH // 2, FH)]
        down_psum = bank(2)[:, 0:EC * P]

        def bank67(j):
            return psum[0:P, bass.ds(6 * 512 + (j % 2) * 512, 512)]

        def tile_of(t):
            return acc[:, bass.ds(t, 1), :].rearrange("p a d -> p (a d)")

        names = """st_psum w_ready den_ready score_step edges_loaded x_loaded wv_loaded wn_loaded wc_loaded
            wo_loaded wf_loaded wu_loaded wd_loaded keys_loaded omega_loaded bias_loaded pair_loaded
            const_ready iota_ready pool_step vec_step edges_float edges_transposed edge_cols_ready cand_ready
            candT_ready cand_max_ready cand_row_ready ranges_ready setup_transposed setup_stored
            stats_ready var_ready rstd_ready xn_ready xnT_psum x_staged xnT_stored v_psum beta_psum
            wc_psum v_stored beta_stored wc_added om_zeroed q_psum k_psum q_stored k_stored fq_psum
            ssq_psum ssk_psum fk_psum fq_min ssq_max ssk_max fk_min fq_exp ssq_exp ssk_exp fk_exp
            kphi_ready qphi_ready kv_psum kv_stored den_psum num_psum den_stored num_stored nk_ready
            attn_ready den_inv mix_step wo_psum wo_added dst_diff dst_square dst_ready adj_done
            adj_stored col_summed count_psum count_inv gnn_psum at_staged mean_copied x1_ready
            x1_stats xn2_ready xn2T_psum xn2T_stored q2_psum q2_stored sim_psum sim_stored hd_psum
            hd_stored gelu_step gelu_u tanh_done gelu_ready topk_step topv_ready all_ready
            negm_ready ex1_done rest_ready topd_ready topd_exp ex2_done diff_ready sel_step
            com_ready out_psum out_copied out_ready out_stored passed
            """.split()
        S = {n: sem(n) for n in names}
        hot_ready = [sem(f"hot_ready{k}") for k in range(CT)]
        hot_free = [sem(f"hot_free{k}") for k in range(CT)]

        def load_range(eng, which, j):
            return eng.value_load(rng_i[0:1, which, bass.ds(j, 1)], min_val=0, max_val=T * NCH)

        @contextmanager
        def slots(eng, j):
            lo = load_range(eng, 0, j)
            hi = load_range(eng, 1, j)
            ch0 = load_range(eng, 2, j)
            with eng.Fori(lo, hi) as slot:
                e0 = nc.s_assert_within((slot - lo + ch0) * CT, 0, (NCH - 1) * CT,
                                        skip_runtime_bounds_check_because="the ranges are clamped to the chunks")
                yield slot, e0

        block = ctx.enter_context(nc.Block())

        @block.sync
        def _(sp):
            sp.dma_start(edges_i[:, 0, :], src.rearrange("(p c) -> p c", p=NCH)).then_inc(S["edges_loaded"], 16)
            sp.dma_start(edges_i[:, 1, :], dst.rearrange("(p c) -> p c", p=NCH)).then_inc(S["edges_loaded"], 16)
            sp.dma_start(acc[:, :, :], x.rearrange("(t p) d -> p t d", p=P)).then_inc(S["x_loaded"], 16)
            for i, (w, s) in enumerate([(Wv, "wv_loaded"), (wn, "wn_loaded"), (wc, "wc_loaded"), (Wo, "wo_loaded")]):
                sp.dma_start(W[:, i], w.rearrange("(k p) d -> p k d", p=128)).then_inc(S[s], 16)
            sp.dma_start(wf_sb[:, :, :], wf.rearrange("(k p) d -> p k d", p=128)).then_inc(S["wf_loaded"], 16)
            wqv = Wq.rearrange("(k p) (c m) -> c p k m", p=128, m=128)
            wkv = Wk.rearrange("(k p) (c m) -> c p k m", p=128, m=128)
            sp.dma_start(w_pair[:, 0], wqv[0]).then_inc(S["pair_loaded"], 16)
            sp.dma_start(w_pair[:, 1], wkv[0]).then_inc(S["pair_loaded"], 16)
            with sp.Fori(1, NPAIR) as c:
                sp.wait_ge(S["k_psum"], c)
                sp.dma_start(w_pair[:, 0], wqv[bass.ds(c, 1)].rearrange("a p k m -> p (a k) m")).then_inc(S["pair_loaded"], 16)
                sp.dma_start(w_pair[:, 1], wkv[bass.ds(c, 1)].rearrange("a p k m -> p (a k) m")).then_inc(S["pair_loaded"], 16)
            outv = out.rearrange("(t p) d -> t p d", p=P)
            with sp.Fori(0, T) as t:
                sp.wait_ge(S["out_ready"], t + 2)
                sp.dma_start(outv[bass.ds(t, 1)].rearrange("a p d -> p (a d)"),
                             acc[:, bass.ds(t, 1), :].rearrange("p a d -> p (a d)")).then_inc(S["out_stored"], 16)
            sp.wait_ge(S["out_stored"], 16 * T)

        @block.gpsimd
        def _(pool):
            g = nc.gpsimd
            step = Steps(pool, S["pool_step"])
            g.memset(ident[:, :], 0.0)
            g.memset(om_qb[:, :], 0.0)
            g.memset(om_kb[:, :], 0.0).then_inc(S["om_zeroed"], 1)
            g.iota(iota[:, :], [[1, N]], base=0, channel_multiplier=0, allow_small_or_imprecise_dtypes=True)
            g.iota(blk_lo[:, :], [[P, T]], base=0, channel_multiplier=0, allow_small_or_imprecise_dtypes=True)
            g.iota(blk_hi[:, :], [[P, T]], base=P, channel_multiplier=0, allow_small_or_imprecise_dtypes=True)
            g.iota(ch_rank[:, 0:1], [[0, 1]], base=1, channel_multiplier=1, allow_small_or_imprecise_dtypes=True)
            g.iota(ch_rank[:, 1:2], [[0, 1]], base=NCH, channel_multiplier=-1, allow_small_or_imprecise_dtypes=True)
            g.memset(zrow[:, :], 0.0)
            g.memset(ones1[:, :], 1.0)
            g.memset(mhalf[:, :], -0.5)
            g.memset(kv_blk[:, :], 0.0)
            g.memset(ones_blk[:, :], 0.0)
            g.memset(pair_ones[:, :], 0.0)
            step.link(g.memset(vaug[:, :, :, VC - 1:VC], 1.0))
            g.memset(pair_ones[0:DH, 0:DH], 1.0)
            step.link(g.memset(pair_ones[DH:128, DH:128], 1.0))
            g.affine_select(out=ident[:, :], in_=ident[:, :], compare_op=ALU.not_equal, fill=1.0,
                            base=0, pattern=[[-1, 128]], channel_multiplier=1).then_inc(S["const_ready"], 1)
            pool.wait_ge(S["om_zeroed"], 1)
            for b in range(2):
                for t_, s_ in ((om_qb, om_q), (om_kb, om_k)):
                    pool.dma_start(t_[b * DH:(b + 1) * DH, b * DH:(b + 1) * DH], s_).then_inc(S["omega_loaded"], 16)
            PS = step.n

            def rstd_of(n):
                hold(pool, S["var_ready"], n + 1, S["passed"])
                g.tensor_scalar(rstd[:, :], ag[:, 1:2], LN_EPS, None, ALU.add).then_inc(S["pool_step"], 1)
                pool.wait_ge(S["pool_step"], PS + 1 + n)
                g.tensor_tensor(rstd[:, :], rstd[:, :], mhalf[:, :], ALU.pow).then_inc(S["rstd_ready"], 1)

            def offsets(j):
                with slots(pool, j) as (slot, e0):
                    side = pool.snap((slot % RING) * CT)
                    pool.wait_ge(S["dst_ready"], 2 * slot + 2)
                    g.tensor_tensor(dst_off[:, bass.ds(side, CT), :],
                                    iota[:, bass.ds(j * P, P)].unsqueeze(1).to_broadcast([P, CT, P]),
                                    edge_cols[:, 1, bass.ds(e0, CT)].unsqueeze(2).to_broadcast([P, CT, P]),
                                    ALU.subtract).then_inc(S["dst_diff"], 1)
                    hold(pool, S["dst_diff"], slot + 1, S["passed"])
                    g.tensor_tensor(dst_off[:, bass.ds(side, CT), :], dst_off[:, bass.ds(side, CT), :],
                                    dst_off[:, bass.ds(side, CT), :], ALU.mult).then_inc(S["dst_square"], 1)

            pool.wait_ge(S["iota_ready"], 1)
            pool.wait_ge(S["ranges_ready"], 1)
            pool.wait_ge(S["edge_cols_ready"], 2)
            with pool.Fori(0, T) as j:
                offsets(j)
                rstd_of(j)

            with pool.Fori(0, NPAIR) as c:
                pool.wait_ge(S["nk_ready"], c + 1)
                pool.wait_ge(S["fk_exp"], c + 1)
                g.tensor_tensor(kphi.rearrange("p t (h m) -> p t h m", h=2),
                                kphi.rearrange("p t (h m) -> p t h m", h=2),
                                nk[:, :, :].unsqueeze(3).to_broadcast([P, T, 2, DH]), ALU.mult)\
                    .then_inc(S["kphi_ready"], 1)

            def gelu_in(t):
                hold(pool, S["hd_stored"], t + 2, S["passed"])
                g.tensor_scalar(hu, hu, GELU_A, 1.0, ALU.mult, ALU.add).then_inc(S["gelu_step"], 1)
                pool.wait_ge(S["gelu_step"], 2 * t + 1)
                g.tensor_tensor(hu, hu, hx, ALU.mult).then_inc(S["gelu_u"], 1)

            def gelu_out(t):
                hold(pool, S["tanh_done"], t + 1, S["passed"])
                g.tensor_scalar(hu, hu, 0.5, 0.5, ALU.mult, ALU.add).then_inc(S["gelu_step"], 1)
                pool.wait_ge(S["gelu_step"], 2 * t + 2)
                g.tensor_tensor(gl[:, bass.ds(t % 2, 1), :].rearrange("p a n -> p (a n)"), hu, hx, ALU.mult)\
                    .then_inc(S["gelu_ready"], 1)

            def add_mean(t):
                if isinstance(t, int):
                    pool.wait_ge(S["wo_added"], (NPAIR - 1) * T + 2 if t == 0 else NPAIR * T + 1)
                pool.wait_ge(S["mean_copied"], t + 1)
                g.tensor_tensor(tile_of(t), tile_of(t), sum_tile, ALU.add).then_inc(S["x1_ready"], 1)

            def add_out(t):
                pool.wait_ge(S["out_copied"], t + 2)
                g.tensor_tensor(tile_of(t), tile_of(t), out_tile, ALU.add).then_inc(S["out_ready"], 1)

            def all_scores(t, half):
                hs = halves[half]
                shp = [P, FH // 2, TOP, TOP]
                pool.wait_ge(S["ex1_done"], t + 1)
                pool.wait_ge(S["topv_ready"], 2 * t + half + 1)
                g.tensor_tensor(allsc[:, hs].rearrange("p h (a b) -> p h a b", a=TOP),
                                topv[:, hs].unsqueeze(3).to_broadcast(shp),
                                topf[:, hs].unsqueeze(2).to_broadcast(shp), ALU.add)\
                    .then_inc(S["all_ready"], 1)

            def diff(t):
                for half in range(2):
                    pool.wait_ge(S["ex2_done"], 2 * t + half + 3)
                    hs = halves[half]
                    g.tensor_tensor(ex1[:, hs], ex1[:, hs], ex2[:, hs], ALU.subtract).then_inc(S["diff_ready"], 1)

            def iteration(t, ahead=True, out=True):
                gelu_in(t)
                if out:
                    add_out(t - 2)
                if ahead:
                    add_mean(t + 2)
                diff(t - 1)
                gelu_out(t)
                if ahead:
                    rstd_of(T + t + 2)
                all_scores(t, 0)
                all_scores(t, 1)

            add_mean(0)
            rstd_of(T)
            gelu_in(0)
            gelu_out(0)
            add_mean(1)
            rstd_of(T + 1)
            all_scores(0, 0)
            all_scores(0, 1)
            add_mean(2)
            rstd_of(T + 2)
            iteration(1, out=False)
            with pool.Fori(2, T - 2) as t:
                iteration(t)
            iteration(T - 2, ahead=False)
            iteration(T - 1, ahead=False)
            add_out(T - 2)

        @block.scalar
        def _(act):
            a = nc.scalar
            for half in range(2):
                act.dma_start(keys_nat[:, half], keys[:, half * 128:(half + 1) * 128, 0, :].rearrange("h p d -> p h d"))\
                    .then_inc(S["keys_loaded"], 16)
            act.dma_start(wd_nat, w_down[0:NE, :].rearrange("(g p) d -> p g d", g=EC)).then_inc(S["wd_loaded"], 16)
            act.dma_start(wu_sb[:, :, :], w_up[0:NE, :].rearrange("(g p) d -> p g d", g=EC)).then_inc(S["wu_loaded"], 16)
            act.dma_start(bias_bc[:, :], bias.rearrange("(a d) -> a d", a=1).to_broadcast([P, D]))\
                .then_inc(S["bias_loaded"], 16)
            act.wait_ge(S["edges_transposed"], 1)
            for s in range(2):
                a.activation(edge_cols[:, s, :].rearrange("q (p a) -> q a p", p=NCH),
                             bank(s)[0:P, 0:CT * NCH].rearrange("q (a p) -> q a p", a=CT),
                             ACT.Copy, scale=UNIT).then_inc(S["edge_cols_ready"], 1)
            def transposed_out(t):
                act.wait_ge(S["xnT_psum"], t + 2)
                act.wait_ge(S["wc_psum"], t + 1)
                a.activation(x_stage[:, :, :], bank(3)[:, 0:KC * P].rearrange("p (k n) -> p k n", k=KC),
                             ACT.Copy).then_inc(S["x_staged"], 1)
                a.activation(xnT3[:, :, bass.ds(t * P, P)], bank(3)[:, 0:KC * P].rearrange("p (k n) -> p k n", k=KC),
                             ACT.Copy).then_inc(S["xnT_stored"], 1)

            def destinations(j):
                with slots(act, j) as (slot, e0):
                    side = act.snap((slot % RING) * CT)
                    turn = act.snap(slot + 1)
                    hold(act, S["dst_square"], turn, S["passed"])
                    for half in range(2):
                        hold(act, hot_free[half * CH + CH - 1], turn, S["passed"])
                        a.activation(hot_dst[:, half * CH:(half + 1) * CH, :],
                                     dst_off[:, bass.ds(side + half * CH, CH), :], ACT.Relu, bias=ones1[:, 0:1],
                                     scale=-1.0 / (UNIT * UNIT)).then_inc(S["dst_ready"], 1)

            def block_out(t):
                act.wait_ge(S["adj_done"], t + 1)
                a.activation(adj[:, bass.ds(t, 1), :], psum[0:P, 0:N], ACT.Copy).then_inc(S["adj_stored"], 1)

            def tile_out(t):
                act.wait_ge(S["v_psum"], t + 1)
                a.activation(vaug[:, bass.ds(t, 1), :, 0:2 * DH].rearrange("p a c v -> p (a c) v"),
                             bank(4)[0:P].rearrange("p (c v) -> p c v", c=NPAIR), ACT.Copy).then_inc(S["v_stored"], 1)
                act.wait_ge(S["beta_psum"], t + 1)
                a.activation(beta[0:P, bass.ds(t, 1), :].rearrange("p a d -> p (a d)"), bank(5)[0:P],
                             ACT.Copy).then_inc(S["beta_stored"], 1)

            act.sem_inc(S["dst_ready"], 2 * RING)
            act.wait_ge(S["ranges_ready"], 1)
            destinations(0)
            block_out(0)
            act.wait_ge(S["setup_transposed"], 1)
            a.activation(keysT[:, :, :], bank(5)[:, 0:2 * NK].rearrange("p (c k) -> p c k", c=2), ACT.Copy)
            a.activation(wdT[:, :, :], bank(6, 2).rearrange("p (c k) -> p c k", c=KC), ACT.Copy)\
                .then_inc(S["setup_stored"], 1)
            destinations(1)
            transposed_out(0)
            with act.Fori(1, T - 1) as t:
                block_out(t)
                destinations(t + 1)
                tile_out(t - 1)
                transposed_out(t)
            block_out(T - 1)
            tile_out(T - 2)
            transposed_out(T - 1)
            tile_out(T - 1)

            def qk_out(c):
                act.wait_ge(S["q_psum"], c + 1)
                a.activation(qT, psum[:, 0:N], ACT.Copy, scale=Q_SCALE)
                a.activation(sqq, psum[:, 0:N], ACT.Square, scale=Q_SCALE).then_inc(S["q_stored"], 1)
                act.wait_ge(S["k_psum"], c + 1)
                a.activation(kT, bank(3, 3)[:, 0:N], ACT.Copy, scale=Q_SCALE)
                a.activation(sqk, bank(3, 3)[:, 0:N], ACT.Square, scale=Q_SCALE).then_inc(S["k_stored"], 1)

            def features_out(c):
                act.wait_ge(S["fk_min"], c + 1)
                a.activation(kphi, kphi, ACT.Exp).then_inc(S["fk_exp"], 1)
                act.wait_ge(S["ssk_max"], c + 1)
                a.activation(nk[:, :, :], nk[:, :, :], ACT.Exp, scale=-0.5).then_inc(S["ssk_exp"], 1)
                act.wait_ge(S["fq_min"], c + 1)
                a.activation(qphi, qphi, ACT.Exp).then_inc(S["fq_exp"], 1)
                act.wait_ge(S["ssq_max"], c + 1)
                a.activation(sqq, sqq, ACT.Exp, scale=-0.5).then_inc(S["ssq_exp"], 1)
                act.wait_ge(S["den_psum"], c + 1)
                a.activation(den_all, psum[:, 0:N], ACT.Copy).then_inc(S["den_stored"], 1)
                act.wait_ge(S["num_psum"], c + 1)
                a.activation(num, bank(3, 3)[:, 0:N], ACT.Copy).then_inc(S["num_stored"], 1)

            qk_out(0)
            with act.Fori(0, NPAIR - 1) as c:
                features_out(c)
                qk_out(c + 1)
            features_out(NPAIR - 1)

            def front_stage(t):
                act.wait_ge(S["gnn_psum"], t + 1)
                a.activation(at_stage, adj[:, :, bass.ds(t * P, P)], ACT.Copy).then_inc(S["at_staged"], 1)

            def down_out(t):
                act.wait_ge(S["hd_psum"], t + 1)
                if not isinstance(t, int) or t > 0:
                    act.wait_ge(S["gelu_ready"], t)
                a.activation(hx, down_psum, ACT.Copy)
                a.activation(hu, down_psum, ACT.Square).then_inc(S["hd_stored"], 1)

            def tanh(t):
                act.wait_ge(S["gelu_u"], t + 1)
                a.activation(hu, hu, ACT.Tanh, scale=GELU_C).then_inc(S["tanh_done"], 1)

            def weigh(t, hs=range(FH)):
                act.wait_ge(S["den_ready"], t + 1)
                for h in hs:
                    if h % (FH // 2) == 0:
                        act.wait_ge(S["diff_ready"], 2 * t + 1 + h // (FH // 2))
                    last = a.activation(ex1[:, h], ex1[:, h], ACT.Copy, scale=rden[:, h:h + 1])
                last.then_inc(S["w_ready"], 1)

            def mean_out(t):
                hold(act, S["gnn_psum"], t + 2, S["passed"])
                if not isinstance(t, int) or t > 0:
                    hold(act, S["x1_ready"], t, S["passed"])
                a.activation(sum_tile, bank(1)[0:P], ACT.Copy, scale=rcnt[:, bass.ds(t, 1)])\
                    .then_inc(S["mean_copied"], 1)

            def out_out(t):
                act.wait_ge(S["out_psum"], t + 1)
                act.wait_ge(S["out_ready"], t + 1)
                a.activation(out_tile, bank(3)[0:P], ACT.Copy).then_inc(S["out_copied"], 1)

            def transposed2_out(t):
                act.wait_ge(S["xn2T_psum"], t + 2)
                a.activation(xn2T, bank(2)[:, 0:KC * P].rearrange("p (k n) -> p k n", k=KC), ACT.Copy)\
                    .then_inc(S["xn2T_stored"], 1)

            def q2_out(t):
                act.wait_ge(S["q2_psum"], t + 1)
                a.activation(q2T, bank(3)[:, 0:KC * P].rearrange("p (k n) -> p k n", k=KC), ACT.Copy,
                             scale=BN_SCALE).then_inc(S["q2_stored"], 1)

            def sim_out(t):
                act.wait_ge(S["sim_psum"], t + 1)
                if not isinstance(t, int) or t > 0:
                    act.wait_ge(S["topv_ready"], 2 * t)
                a.activation(sim.rearrange("p (c b) e -> p b c e", c=2),
                             bank(4, 4)[0:P].rearrange("p (b c e) -> p b c e", b=4, c=2), ACT.Copy)\
                    .then_inc(S["sim_stored"], 1)

            def exp_all(t):
                act.wait_ge(S["negm_ready"], t + 1)
                act.wait_ge(S["st_psum"], t + 1)
                for h in range(FH):
                    last = a.activation(ex1[:, h], allsc[:, h], ACT.Exp, bias=negm[:, h:h + 1])
                last.then_inc(S["ex1_done"], 1)
                act.wait_ge(S["topd_ready"], t + 1)
                a.activation(topd, topd, ACT.Exp).then_inc(S["topd_exp"], 1)

            def exp_rest(t):
                for half in range(2):
                    act.wait_ge(S["rest_ready"], 2 * t + half + 1)
                    for h in heads[half]:
                        last = a.activation(ex2[:, h], rest[:, h], ACT.Exp, bias=negm[:, h:h + 1])
                    last.then_inc(S["ex2_done"], 1)

            def iteration(t, ahead=True, staged=True, mean=True, out=True):
                if out:
                    out_out(t - 2)
                if ahead:
                    transposed2_out(t + 1)
                if mean:
                    mean_out(t + 2)
                exp_rest(t - 1)
                tanh(t)
                if ahead:
                    q2_out(t + 1)
                weigh(t - 1)
                if staged:
                    front_stage(t + 3)
                if ahead:
                    down_out(t + 1)
                    sim_out(t + 1)
                exp_all(t)

            for n, credit in (("hd_stored", 1), ("q2_stored", 1), ("sim_stored", 1), ("ex1_done", 1), ("ex2_done", 2),
                              ("out_copied", 1)):
                act.sem_inc(S[n], credit)
            front_stage(0)
            act.wait_ge(S["count_inv"], 1)
            mean_out(0)
            front_stage(1)
            transposed2_out(0)
            q2_out(0)
            down_out(0)
            act.wait_ge(S["wo_psum"], NPAIR * T)
            sim_out(0)
            tanh(0)
            mean_out(1)
            front_stage(2)
            mean_out(2)
            transposed2_out(1)
            q2_out(1)
            front_stage(3)
            down_out(1)
            sim_out(1)
            exp_all(0)
            iteration(1, out=False)
            with act.Fori(2, T - 3) as t:
                iteration(t)
            iteration(T - 3, staged=False)
            iteration(T - 2, staged=False, mean=False)
            iteration(T - 1, ahead=False, staged=False, mean=False)
            exp_rest(T - 1)
            weigh(T - 1, heads[0])
            out_out(T - 2)

        @block.vector
        def _(dve):
            v = nc.vector
            step = Steps(dve, S["vec_step"])
            dve.wait_ge(S["edges_loaded"], 32)
            v.tensor_copy(edges_f, edges_i).then_inc(S["edges_float"], 1)
            dve.wait_ge(S["edges_float"], 1)
            v.tensor_reduce(ch_lim[:, 0:1], edges_f[:, 1, :], axis=AX.X, op=ALU.min)
            step.link(v.tensor_reduce(ch_lim[:, 1:2], edges_f[:, 1, :], axis=AX.X, op=ALU.max))
            dve.wait_ge(S["const_ready"], 1)
            shp = [NCH, T]
            v.tensor_tensor(touch[:, 0], blk_hi[:, :], ch_lim[:, 0:1].to_broadcast(shp), ALU.is_gt)
            step.link(v.tensor_tensor(touch[:, 1], blk_lo[:, :], ch_lim[:, 1:2].to_broadcast(shp), ALU.is_le))
            step.link(v.tensor_tensor(touch[:, 2], touch[:, 0], touch[:, 1], ALU.mult))
            v.tensor_tensor(cand[:, 0], touch[:, 2], ch_rank[:, 0:1].to_broadcast(shp), ALU.mult)
            v.tensor_tensor(cand[:, 1], touch[:, 2], ch_rank[:, 1:2].to_broadcast(shp), ALU.mult)\
                .then_inc(S["cand_ready"], 1)
            v.tensor_scalar(iota[:, :], iota[:, :], UNIT, None, ALU.mult).then_inc(S["iota_ready"], 1)
            dve.wait_ge(S["candT_ready"], 1)
            v.reduce_max(cand_max[:, :], bank(5)[0:2 * T, 0:NCH], AX.X).then_inc(S["cand_max_ready"], 1)
            dve.wait_ge(S["cand_row_ready"], 1)
            step.link(v.tensor_copy(rng[0:1, 0:2, :], bank(6)[0:1, 0:2 * T].rearrange("p (k j) -> p k j", k=2)))
            step.link(v.tensor_scalar(rng[0:1, 7, :], rng[0:1, 1, :], 1.0, -1.0, ALU.max, ALU.mult))
            v.tensor_scalar(rng[0:1, 2, :], rng[0:1, 7, :], float(NCH), None, ALU.add)
            step.link(v.tensor_scalar(rng[0:1, 3, :], rng[0:1, 7, :], float(NCH + 1), None, ALU.add))
            step.link(v.tensor_tensor(rng[0:1, 3, :], rng[0:1, 3, :], rng[0:1, 0, :], ALU.max))
            step.link(v.tensor_tensor(rng[0:1, 4, :], rng[0:1, 3, :], rng[0:1, 2, :], ALU.subtract))
            step.link(v.tensor_tensor_scan(rng[0:1, 5, :], rng[0:1, 4, :], rng[0:1, 4, :], 0.0, ALU.add, ALU.max))
            step.link(v.tensor_tensor(rng[0:1, 6, :], rng[0:1, 5, :], rng[0:1, 4, :], ALU.subtract))
            v.tensor_copy(rng_i[0:1, 0, :], rng[0:1, 6, :])
            v.tensor_copy(rng_i[0:1, 1, :], rng[0:1, 5, :])
            v.tensor_copy(rng_i[0:1, 2, :], rng[0:1, 2, :]).then_inc(S["ranges_ready"], 1)

            dve.wait_ge(S["ranges_ready"], 1)
            dve.wait_ge(S["iota_ready"], 1)
            dve.wait_ge(S["edge_cols_ready"], 2)
            for k in range(CT):
                dve.sem_inc(hot_ready[k], 1)
            dve.sem_inc(S["wc_added"], 1)
            def statistics(j):
                v.bn_stats(st[:, :], tile_of(j)).then_inc(S["stats_ready"], 1)
                hold(dve, S["stats_ready"], j + 1, S["passed"])
                v.bn_aggr(ag[:, :], st[:, :]).then_inc(S["var_ready"], 1)

            def normalised(j):
                at = tile_of(j)
                dve.wait_ge(S["xnT_psum"], j + 1)
                dve.wait_ge(S["rstd_ready"], j + 1)
                v.tensor_scalar(xn_tile, at, ag[:, 0:1], rstd[:, :], ALU.subtract, ALU.mult)\
                    .then_inc(S["xn_ready"], 1)
                dve.wait_ge(S["xn_ready"], j + 1)
                v.tensor_tensor(at, at, bias_bc[:, :], ALU.add).then_inc(S["mix_step"], 1)

            def one_hots(j):
                with slots(dve, j) as (slot, e0):
                    for k in range(CT):
                        if k % 2 == 0:
                            dve.wait_ge(hot_free[k + 1], slot + 1)
                        v.tensor_scalar(hot_src[:, k, :], iota[:, :], edge_cols[:, 0, bass.ds(e0 + k, 1)], None,
                                        ALU.is_equal).then_inc(hot_ready[k], 1)

            def add_wc(j):
                dve.wait_ge(S["mix_step"], j + 1)
                dve.wait_ge(S["wc_psum"], j + 2)
                v.tensor_tensor(tile_of(j), tile_of(j), bank67(j), ALU.add).then_inc(S["wc_added"], 1)

            one_hots(0)
            dve.wait_ge(S["x_loaded"], 16)
            dve.wait_ge(S["bias_loaded"], 16)
            statistics(0)
            normalised(0)
            one_hots(1)
            statistics(1)
            normalised(1)
            with dve.Fori(2, T) as j:
                one_hots(j)
                statistics(j)
                add_wc(j - 2)
                normalised(j)
            add_wc(T - 2)
            add_wc(T - 1)
            dve.wait_ge(S["adj_stored"], T + 1)
            v.reduce_sum(col_sum[:, :], adj[:, :, :].rearrange("p t n -> p n t"), AX.X).then_inc(S["col_summed"], 1)

            def add_wo(c, ts):
                for t in ts:
                    dve.wait_ge(S["wo_psum"], c * T + t + 1)
                    if t == 0:
                        dve.wait_ge(S["wo_added"], c * T + 1)
                    v.tensor_tensor(acc[:, t, :], acc[:, t, :], bank(6 + t % 2)[0:P], ALU.add)\
                        .then_inc(S["wo_added"], 1)

            def features(c, first=False):
                dve.wait_ge(S["fq_psum"], c + 1)
                v.tensor_scalar(qphi, psum[:, 0:N], CLAMP, None, ALU.min).then_inc(S["fq_min"], 1)
                dve.wait_ge(S["fk_psum"], c + 1)
                v.tensor_scalar(kphi, bank(3, 3)[0:P, 0:T * 128].rearrange("p (t m) -> p t m", t=T), CLAMP, None,
                                ALU.min).then_inc(S["fk_min"], 1)
                dve.wait_ge(S["ssk_psum"], c + 1)
                v.tensor_scalar(nk[:, :, :], bank(6)[0:P, 0:2 * T].rearrange("p (t h) -> p t h", h=2), EPS * EPS,
                                None, ALU.max).then_inc(S["ssk_max"], 1)
                dve.wait_ge(S["ssq_psum"], c + 1)
                v.tensor_scalar(sqq, psum[:, 0:N], EPS * EPS, None, ALU.max).then_inc(S["ssq_max"], 1)
                if not first:
                    add_wo(c - 1, range(0, 3))
                dve.wait_ge(S["ssk_exp"], c + 1)
                v.tensor_scalar(nk[:, :, :], nk[:, :, :], EPS, None, ALU.max).then_inc(S["nk_ready"], 1)
                if not first:
                    add_wo(c - 1, range(3, 5))
                dve.wait_ge(S["ssq_exp"], c + 1)
                dve.wait_ge(S["fq_exp"], c + 1)
                v.scalar_tensor_tensor(qphi, sqq, EPS, qphi, ALU.max, ALU.mult).then_inc(S["qphi_ready"], 1)
                if not first:
                    add_wo(c - 1, range(5, T))
                dve.wait_ge(S["kv_psum"], c + 1)
                kv = bank(6)
                v.tensor_copy(kv_blk[0:DH, 0:DH], kv[0:DH, 0:DH])
                v.tensor_copy(kv_blk[DH:128, DH:128], kv[DH:128, DH:2 * DH])
                v.tensor_copy(ones_blk[0:DH, 0:DH], kv[0:DH, VC - 1:VC].to_broadcast([DH, DH]))
                v.tensor_copy(ones_blk[DH:128, DH:128], kv[DH:128, VC - 1:VC].to_broadcast([DH, DH]))\
                    .then_inc(S["kv_stored"], 1)
                dve.wait_ge(S["den_stored"], c + 1)
                v.reciprocal(den_all, den_all).then_inc(S["den_inv"], 1)
                dve.wait_ge(S["den_inv"], c + 1)
                dve.wait_ge(S["num_stored"], c + 1)
                v.tensor_tensor(num, num, den_all, ALU.mult).then_inc(S["attn_ready"], 1)

            features(0, first=True)
            with dve.Fori(1, NPAIR) as c:
                features(c)
            dve.wait_ge(S["count_psum"], 1)
            v.reciprocal(rcnt[:, :], bank(2)[0:P, 512 - T:512]).then_inc(S["count_inv"], 1)


            class Norm2:

                def __init__(self, t):
                    self.t, self.at = t, tile_of(t)

                def stats(self):
                    hold(dve, S["x1_ready"], self.t + 1, S["passed"])
                    v.bn_stats(st[:, :], self.at).then_inc(S["x1_stats"], 1)

                def aggregate(self):
                    if not isinstance(self.t, int) or self.t > 0:
                        hold(dve, S["xn2_ready"], self.t, S["passed"])
                    hold(dve, S["x1_stats"], self.t + 1, S["passed"])
                    v.bn_aggr(ag[:, :], st[:, :]).then_inc(S["var_ready"], 1)

                def normalise(self):
                    dve.wait_ge(S["xn2T_psum"], self.t + 1)
                    dve.wait_ge(S["rstd_ready"], T + self.t + 1)
                    v.tensor_scalar(xn_tile, self.at, ag[:, 0:1], rstd[:, :], ALU.subtract, ALU.mult)\
                        .then_inc(S["xn2_ready"], 1)

            KS = 10

            def top_keys(t, between):
                stages = [lambda h: v.max(topv[:, h, 0:8], sim[:, h]),
                          lambda h: v.max_index(topi[:, h, 0:8], topv[:, h, 0:8], sim[:, h]),
                          lambda h: v.match_replace(sim[:, h], topv[:, h, 0:8], sim[:, h], LOWEST),
                          lambda h: v.max(topv[:, h, 8:16], sim[:, h]),
                          lambda h: v.max_index(topi[:, h, 8:16], topv[:, h, 8:16], sim[:, h])]
                hold(dve, S["sim_stored"], t + 2, S["passed"])
                if not isinstance(t, int) or t > 0:
                    hold(dve, S["all_ready"], 2 * t, S["passed"])
                for n, stage in enumerate(stages):
                    for half in range(2):
                        if n:
                            hold(dve, S["topk_step"], KS * t + 2 * n - 1 + half, S["passed"])
                        for h in heads[half]:
                            last = stage(h)
                        last.then_inc(S["topk_step"], 1)
                        for step_ in between.get((n, half), []):
                            step_()
                        if n == len(stages) - 1:
                            dve.wait_ge(S["topk_step"], KS * t + KS - 1 + half)
                            hs = halves[half]
                            v.tensor_copy(topf[:, hs], topi[:, hs]).then_inc(S["topv_ready"], 1)

            SS = 6

            def top_scores(t, den_of=None):
                for half in range(2):
                    hold(dve, S["all_ready"], 2 * t + half + 1, S["passed"])
                    for h in heads[half]:
                        last = v.max(tops[:, h, 0:8], allsc[:, h])
                    last.then_inc(S["score_step"], 1)
                hold(dve, S["ex2_done"], 2 * t + 2, S["passed"])
                for half in range(2):
                    hold(dve, S["score_step"], SS * t + 1 + half, S["passed"])
                    if half:
                        v.tensor_scalar(negm, tops[:, :, 0], -1.0, None, ALU.mult).then_inc(S["negm_ready"], 1)
                    for h in heads[half]:
                        last = v.match_replace(rest[:, h], tops[:, h, 0:8], allsc[:, h], LOWEST)
                    last.then_inc(S["score_step"], 1)
                for half in range(2):
                    hold(dve, S["score_step"], SS * t + 3 + half, S["passed"])
                    for h in heads[half]:
                        last = v.max(tops[:, h, 8:16], rest[:, h])
                    last.then_inc(S["score_step"], 1)
                    if half == 0 and den_of is not None:
                        combine(den_of)
                for half in range(2):
                    hold(dve, S["score_step"], SS * t + 5 + half, S["passed"])
                    if half:
                        v.tensor_tensor(topd, tops, negm.unsqueeze(2).to_broadcast([P, FH, TOP]), ALU.add)\
                            .then_inc(S["topd_ready"], 1)
                    for h in heads[half]:
                        last = v.match_replace(rest[:, h], tops[:, h, 8:16], rest[:, h], LOWEST)
                    last.then_inc(S["rest_ready"], 1)

            def den_sum(t):
                dve.wait_ge(S["topd_exp"], t + 1)
                v.reduce_sum(den, topd, AX.X).then_inc(S["sel_step"], 1)

            def den_invert(t):
                dve.wait_ge(S["sel_step"], t + 1)
                v.reciprocal(rden, den).then_inc(S["den_ready"], 1)

            def combine(t):
                if not isinstance(t, int) or t > 0:
                    dve.wait_ge(S["out_psum"], t)
                dve.wait_ge(S["st_psum"], t + 2)
                dve.wait_ge(S["gelu_ready"], t + 1)
                v.tensor_tensor(comT.rearrange("p k n -> p (k n)"), bank(0)[:, 0:EC * P],
                                gl[:, bass.ds(t % 2, 1), :].rearrange("p a n -> p (a n)"), ALU.mult)\
                    .then_inc(S["com_ready"], 1)

            def add_out(t):
                dve.wait_ge(S["out_ready"], t + 1)
                dve.wait_ge(S["out_psum"], t + 1)
                v.tensor_tensor(tile_of(t), tile_of(t), bank(3)[0:P], ALU.add).then_inc(S["out_ready"], 1)

            dve.sem_inc(S["out_ready"], 1)
            add_wo(NPAIR - 1, range(1))
            r = Norm2(0)
            add_wo(NPAIR - 1, range(1, 2))
            r.stats()
            add_wo(NPAIR - 1, range(2, 3))
            r.aggregate()
            add_wo(NPAIR - 1, range(3, 5))
            r.normalise()
            add_wo(NPAIR - 1, range(5, T))

            def tile(t, norm=2, den_of=None):
                between = {}

                def put(n, half, f):
                    between.setdefault((n, half), []).append(f)

                if den_of is not None:
                    put(1, 0, lambda: den_sum(den_of))
                    put(1, 1, lambda: den_invert(den_of))
                if norm:
                    r = Norm2(t + norm)
                    put(3, 0, r.stats)
                    put(3, 1, r.aggregate)
                top_keys(t, between)
                if norm:
                    r.normalise()
                top_scores(t, den_of)

            tile(0, norm=1)
            r = Norm2(2)
            for step_ in (r.stats, r.aggregate, r.normalise):
                step_()
            tile(1, den_of=0)
            with dve.Fori(2, T - 2) as t:
                tile(t, den_of=t - 1)
            tile(T - 2, norm=0, den_of=T - 3)
            tile(T - 1, norm=0, den_of=T - 2)
            den_sum(T - 1)
            den_invert(T - 1)
            for half in range(2):
                dve.wait_ge(S["ex2_done"], 2 * T + half + 1)
                hs = halves[half]
                v.tensor_tensor(ex1[:, hs], ex1[:, hs], ex2[:, hs], ALU.subtract).then_inc(S["diff_ready"], 1)
            dve.wait_ge(S["diff_ready"], 2 * T)
            dve.wait_ge(S["den_ready"], T)
            v.tensor_tensor(ex1[:, halves[1]], ex1[:, halves[1]],
                            rden[:, halves[1]].unsqueeze(2).to_broadcast([P, FH // 2, NE]), ALU.mult)\
                .then_inc(S["w_ready"], 1)
            combine(T - 1)
            add_out(T - 1)

        @block.tensor
        def _(pe):
            te = nc.tensor
            pe.wait_ge(S["const_ready"], 1)
            pe.wait_ge(S["edges_float"], 1)
            for s in range(2):
                for k in range(CT):
                    last = te.transpose(bank(s)[0:P, k * NCH:(k + 1) * NCH], edges_f[:, s, k * P:(k + 1) * P],
                                        ident[0:NCH, 0:NCH])
            last.then_inc(S["edges_transposed"], 1)
            pe.wait_ge(S["cand_ready"], 1)
            te.transpose(bank(5)[0:2 * T, 0:NCH], cand[:, :, :].rearrange("p k j -> p (k j)"),
                         ident[0:NCH, 0:NCH]).then_inc(S["candT_ready"], 1)
            pe.wait_ge(S["cand_max_ready"], 1)
            te.transpose(bank(6)[0:1, 0:2 * T], cand_max[:, :], ident[0:2 * T, 0:2 * T])\
                .then_inc(S["cand_row_ready"], 1)
            pe.wait_ge(S["edge_cols_ready"], 2)
            pe.wait_ge(S["ranges_ready"], 1)
            for s in ("xnT_psum", "wc_psum", "v_stored", "beta_stored", "xnT_stored", "adj_stored", "wc_added"):
                pe.sem_inc(S[s], 1)
            for k in range(CT):
                pe.sem_inc(hot_free[k], 1)

            def transposed(j):
                pe.wait_ge(S["xn_ready"], j + 1)
                pe.wait_ge(S["xnT_stored"], j + 1)
                for k in range(KC):
                    last = te.transpose(bank(3)[:, k * P:(k + 1) * P], xn_tile[:, k * 128:(k + 1) * 128],
                                        ident[0:P, 0:P])
                last.then_inc(S["xnT_psum"], 1)

            def adjacency(j):
                lo = load_range(pe, 0, j)
                hi = load_range(pe, 1, j)
                pe.wait_ge(S["adj_stored"], j + 1)
                for lo_, hi_ in banks:
                    te.matmul(psum[0:P, lo_:hi_], zrow[0:1, 0:P], zrow[0:1, 0:hi_ - lo_], start=True, stop=False)
                with pe.Fori(lo, hi) as slot:
                    for k in range(CT):
                        if k % CH == 0:
                            pe.wait_ge(S["dst_ready"], 2 * slot + k // CH + 1 + 2 * RING)
                        pe.wait_ge(hot_ready[k], slot + 2)
                        for lo_, hi_ in banks:
                            last = te.matmul(psum[0:P, lo_:hi_], hot_dst[:, k, :], hot_src[:, k, lo_:hi_],
                                             start=False, stop=False)
                        last.then_inc(hot_free[k], 1)
                for lo_, hi_ in banks:
                    last = te.matmul(psum[0:P, lo_:lo_ + 1], zrow[0:1, 0:P], zrow[0:1, 0:1], start=False, stop=True)
                last.then_inc(S["adj_done"], 1)

            def token_products(j):
                pe.wait_ge(S["x_staged"], j + 1)
                for to, w, s, free in ((bank(4)[0:P], Wv_sb, "v_psum", "v_stored"),
                                       (bank(5)[0:P], wn_sb, "beta_psum", "beta_stored"),
                                       (bank67(j), wc_sb, "wc_psum", "wc_added")):
                    pe.wait_ge(S[free], j + 1)
                    for k in range(KC):
                        last = te.matmul(to, x_stage[:, k, :], w[:, k, :], start=(k == 0), stop=(k == KC - 1))
                    last.then_inc(S[s], 1)

            adjacency(0)
            pe.wait_ge(S["keys_loaded"], 32)
            for c in range(2):
                for gk in range(2):
                    te.transpose(bank(5)[:, c * NK + gk * 128:c * NK + (gk + 1) * 128],
                                 keys_nat[:, gk, 4 * c:4 * c + 4, :].rearrange("p h d -> p (h d)"), ident[:, :])
            pe.wait_ge(S["wd_loaded"], 16)
            for c in range(KC):
                for gk in range(EC):
                    last = te.transpose(bank(6, 2)[:, c * NE + gk * 128:c * NE + (gk + 1) * 128],
                                        wd_nat[:, gk, c * 128:(c + 1) * 128], ident[:, :])
            last.then_inc(S["setup_transposed"], 1)
            transposed(0)
            adjacency(1)
            pe.wait_ge(S["setup_stored"], 1)
            pe.wait_ge(S["wv_loaded"], 16)
            pe.wait_ge(S["wn_loaded"], 16)
            pe.wait_ge(S["wc_loaded"], 16)
            token_products(0)
            with pe.Fori(1, T - 1) as j:
                transposed(j)
                adjacency(j + 1)
                token_products(j)
            transposed(T - 1)
            token_products(T - 1)

            pe.wait_ge(S["xnT_stored"], T + 1)
            pe.wait_ge(S["v_stored"], T + 1)
            pe.wait_ge(S["beta_stored"], T + 1)
            pe.wait_ge(S["wc_added"], T + 2)
            pe.wait_ge(S["adj_stored"], T + 1)
            pe.wait_ge(S["omega_loaded"], 64)
            pe.wait_ge(S["wo_loaded"], 16)
            pe.sem_inc(S["wo_added"], 1)

            def project(c):
                pe.wait_ge(S["pair_loaded"], c * 32 + 32)
                for i, s in enumerate(("q_psum", "k_psum")):
                    if not isinstance(c, int) or c > 0:
                        pe.wait_ge(S[("den_stored", "num_stored")[i]], c)
                    for lo_, hi_ in banks:
                        for k in range(KC):
                            last = te.matmul(bank(3 * i, 3)[:, lo_:hi_], w_pair[:, i, k, :], xnT3[:, k, lo_:hi_],
                                             start=(k == 0), stop=(k == KC - 1))
                    last.then_inc(S[s], 1)

            def feature_products(c):
                pe.wait_ge(S["q_stored"], c + 1)
                for lo_, hi_ in banks:
                    last = te.matmul(psum[:, lo_:hi_], om_qb[:, :], qT[:, lo_:hi_], start=True, stop=True)
                last.then_inc(S["fq_psum"], 1)
                pe.wait_ge(S["k_stored"], c + 1)
                for t in range(T):
                    last = te.matmul(bank(3, 3)[0:P, t * 128:(t + 1) * 128], kT[:, t * P:(t + 1) * P], om_kb[:, :],
                                     start=True, stop=True)
                last.then_inc(S["fk_psum"], 1)
                if not isinstance(c, int) or c > 1:
                    pe.wait_ge(S["wo_added"], (c - 1) * T + 1)
                for t in range(T):
                    last = te.matmul(bank(6)[0:P, 2 * t:2 * t + 2], sqk[:, t * P:(t + 1) * P],
                                     pair_ones[:, DH - 1:DH + 1], start=True, stop=True)
                last.then_inc(S["ssk_psum"], 1)
                pe.wait_ge(S["fq_min"], c + 1)
                for lo_, hi_ in banks:
                    last = te.matmul(psum[:, lo_:hi_], pair_ones[:, :], sqq[:, lo_:hi_], start=True, stop=True)
                last.then_inc(S["ssq_psum"], 1)

            def attention(c):
                pe.wait_ge(S["kphi_ready"], c + 1)
                if not isinstance(c, int) or c > 0:
                    pe.wait_ge(S["wo_added"], c * T)
                for t in range(T):
                    last = te.matmul(bank(6)[:, 0:VC], kphi[:, t, :],
                                     vaug[:, t, bass.ds(c, 1), :].rearrange("p a v -> p (a v)"),
                                     start=(t == 0), stop=(t == T - 1))
                last.then_inc(S["kv_psum"], 1)
                pe.wait_ge(S["kv_stored"], c + 1)
                pe.wait_ge(S["qphi_ready"], c + 1)
                for to, w, s in ((psum, ones_blk, "den_psum"), (bank(3, 3), kv_blk, "num_psum")):
                    for lo_, hi_ in banks:
                        last = te.matmul(to[:, lo_:hi_], w[:, :], qphi[:, lo_:hi_], start=True, stop=True)
                    last.then_inc(S[s], 1)

            def output(c):
                if not isinstance(c, int) or c < NPAIR - 1:
                    pe.wait_ge(S["ssk_max"], c + 2)
                pe.wait_ge(S["attn_ready"], c + 1)
                for t in range(T):
                    if t >= 2:
                        pe.wait_ge(S["wo_added"], c * T + t)
                    te.matmul(bank(6 + t % 2)[0:P], num[:, t * P:(t + 1) * P],
                              Wo_sb[:, bass.ds(c, 1), :].rearrange("p a d -> p (a d)"),
                              start=True, stop=True).then_inc(S["wo_psum"], 1)

            project(0)
            feature_products(0)
            attention(0)
            project(1)
            with pe.Fori(1, NPAIR - 1) as c:
                feature_products(c)
                output(c - 1)
                attention(c)
                project(c + 1)
            feature_products(NPAIR - 1)
            output(NPAIR - 2)
            attention(NPAIR - 1)

            def gnn(t, between=None):
                pe.wait_ge(S["at_staged"], t + 1)
                if not isinstance(t, int) or t > 0:
                    pe.wait_ge(S["mean_copied"], t)
                for j in range(T):
                    if j == T // 2 and between is not None:
                        between()
                    last = te.matmul(bank(1)[0:P], at_stage[:, j, :], beta[0:P, j, :], start=(j == 0), stop=(j == T - 1))
                last.then_inc(S["gnn_psum"], 1)

            def front(t):
                pe.wait_ge(S["xn2_ready"], t + 1)
                pe.wait_ge(S["hd_stored"], t + 1)
                for k in range(KC):
                    last = te.transpose(bank(2)[:, k * P:(k + 1) * P], xn_tile[:, k * 128:(k + 1) * 128],
                                        ident[0:P, 0:P])
                last.then_inc(S["xn2T_psum"], 1)
                if not isinstance(t, int) or t > 1:
                    pe.wait_ge(S["out_copied"], t - 1)
                pe.wait_ge(S["xn2T_stored"], t + 1)
                for m in range(KC):
                    for k in range(KC):
                        last = te.matmul(bank(3)[:, m * P:(m + 1) * P], wf_sb[:, k, m * 128:(m + 1) * 128],
                                         xn2T[:, k, :], start=(k == 0), stop=(k == KC - 1))
                last.then_inc(S["q2_psum"], 1)
                pe.wait_ge(S["q2_stored"], t + 2)
                pe.wait_ge(S["sim_stored"], t + 1)
                if isinstance(t, int) and t == 0:
                    pe.wait_ge(S["wo_added"], NPAIR * T + 1)
                for h in range(FH):
                    c, b = h // 4, h % 4
                    last = te.matmul(bank(4 + b)[0:P, c * NK:(c + 1) * NK], q2T[b * DK:(b + 1) * DK, c, :],
                                     keysT[b * DK:(b + 1) * DK, c, :], start=True, stop=True)
                last.then_inc(S["sim_psum"], 1)
                for g in range(EC):
                    for k in range(KC):
                        last = te.matmul(down_psum[:, g * P:(g + 1) * P], wdT[:, k, g * 128:(g + 1) * 128],
                                         q2T[:, k, :], start=(k == 0), stop=(k == KC - 1))
                last.then_inc(S["hd_psum"], 1)

            def sum_heads(t):
                pe.wait_ge(S["w_ready"], T + 1 if isinstance(t, int) and t == T - 1 else t + 1)
                for g in range(EC):
                    for h in range(FH):
                        last = te.matmul(bank(0)[:, g * P:(g + 1) * P], ex1[:, h, g * 128:(g + 1) * 128],
                                         ident[0:P, 0:P], start=(h == 0), stop=(h == FH - 1))
                last.then_inc(S["st_psum"], 1)

            def outputs(t):
                pe.wait_ge(S["com_ready"], t + 1)
                pe.wait_ge(S["out_copied"], t + 1)
                for k in range(EC):
                    last = te.matmul(bank(3)[0:P], comT[:, k, :], wu_sb[:, k, :], start=(k == 0), stop=(k == EC - 1))
                last.then_inc(S["out_psum"], 1)

            pe.wait_ge(S["wf_loaded"], 16)
            pe.wait_ge(S["wu_loaded"], 16)
            pe.wait_ge(S["den_stored"], NPAIR)
            pe.sem_inc(S["gnn_psum"], 1)
            pe.sem_inc(S["xn2T_psum"], 1)
            pe.sem_inc(S["st_psum"], 1)
            pe.wait_ge(S["col_summed"], 1)
            for t in range(T):
                last = te.matmul(bank(2)[0:P, 512 - T + t:512 - T + t + 1], col_sum[:, t * P:(t + 1) * P], ones1[:, 0:1],
                                 start=True, stop=True)
            last.then_inc(S["count_psum"], 1)
            gnn(0)
            output(NPAIR - 1)
            front(0)
            gnn(1)
            gnn(2)
            front(1)
            gnn(3)
            with pe.Fori(1, T - 3) as t:
                front(t + 1)
                gnn(t + 3, between=lambda: sum_heads(t - 1))
                outputs(t - 1)
            for t in range(T - 3, T + 1):
                if t < T - 1:
                    front(t + 1)
                sum_heads(t - 1)
                outputs(t - 1)


_INS = ["x", "src", "dst", "L0_gnn_wc", "L0_gnn_wn", "L0_gnn_bias", "L0_mix_Wq", "L0_mix_Wk", "L0_mix_Wv", "L0_mix_Wo",
        "L0_mix_omega_q", "L0_mix_omega_k", "L0_ffn_w_q", "L0_ffn_keys", "L0_ffn_weight_down_embed",
        "L0_ffn_weight_up_embed"]


def kernel(**inputs):
    import numpy as _np
    import concourse.bacc as _bacc
    from concourse import mybir as _mybir
    from concourse.bass_utils import run_bass_kernel_spmd as _run

    nc = _bacc.Bacc("TRN2", target_bir_lowering=False, num_devices=1)
    arrays, args = {}, []
    for name in _INS:
        a = _np.ascontiguousarray(inputs[name])
        arrays[f"in_{name}_dram"] = a
        args.append(nc.dram_tensor(f"in_{name}_dram", a.shape, _mybir.dt.from_np(a.dtype), kind="ExternalInput").ap())
    shape = inputs["x"].shape
    out = nc.dram_tensor("out_dram", shape, _mybir.dt.float32, kind="ExternalOutput").ap()
    gps_layer(nc, *args, out)
    r = _run(nc, [arrays], core_ids=[0])
    return r.results[0]["out_dram"]
```
